# Optimizing a Trainium2 kernel written in Bass

```python
import numpy as np
import jax
import jax.numpy as jnp

def _softmax(x, axis=-1):
    return jax.nn.softmax(x, axis=axis)

def _gelu(x):
    return jax.nn.gelu(x, approximate=True)

def _silu(x):
    return jax.nn.silu(x)

def _sigmoid(x):
    return jax.nn.sigmoid(x)

def _layernorm(x, axis=-1, eps=1e-05):
    m = jnp.mean(x, axis=axis, keepdims=True)
    v = jnp.var(x, axis=axis, keepdims=True)
    return (x - m) / jnp.sqrt(v + eps)

def _scatter_add(tgt, idx, src, axis=0):
    return tgt.at[idx].add(src)

def _segment_sum(src, seg, n):
    return jax.ops.segment_sum(src, seg, n)
kernel_name = 'mk_recurrent_d1_jaxref_r8_2f2a8e'

def setup_inputs(seed: int=0):
    np.random.seed(seed)
    _w = jnp.asarray

    def _L0_attn_setup():
        import jax, jax.numpy as jnp
        import numpy as np
        H = 512
        D = 1024
        N = 16
        K = 4
        R = 32
        BATCH = 1
        L = 256
        EPS = 1e-06

        def _rmsnorm(x, w):
            return x * jax.lax.rsqrt(jnp.mean(x * x, axis=-1, keepdims=True) + EPS) * w
        key = jax.random.key(seed)
        ks = jax.random.split(key, 10)
        s = 0.02
        return {'hidden_states': jax.random.normal(ks[0], (BATCH, L, H), jnp.float32), 'W_in': jax.random.normal(ks[1], (2 * D, H), jnp.float32) * s, 'conv_w': jax.random.normal(ks[2], (D, K), jnp.float32) * s, 'conv_b': jax.random.normal(ks[3], (D,), jnp.float32) * s, 'Wx': jax.random.normal(ks[4], (R + 2 * N, D), jnp.float32) * s, 'dt_ln_w': jnp.ones((R,), jnp.float32), 'b_ln_w': jnp.ones((N,), jnp.float32), 'c_ln_w': jnp.ones((N,), jnp.float32), 'Wdt': jax.random.normal(ks[5], (D, R), jnp.float32) * s, 'dt_bias': jax.random.normal(ks[6], (D,), jnp.float32) * s, 'A': -jnp.exp(jax.random.normal(ks[7], (D, N), jnp.float32) * 0.5), 'D_param': jnp.ones((D,), jnp.float32), 'W_out': jax.random.normal(ks[8], (H, D), jnp.float32) * s}
    _L0_attn_in = _L0_attn_setup()

    def _L0_ffn_setup():
        import jax, jax.numpy as jnp
        import numpy as np
        NUM_EXPERTS = 8
        D_IN = 512
        D_OUT = 512
        key = jax.random.key(seed)
        k_x, k_gw, k_gb, k_ew, k_eb = jax.random.split(key, 5)
        x = jax.random.normal(k_x, (4, 256, D_IN), dtype=jnp.float32)
        gate_w = jax.random.normal(k_gw, (NUM_EXPERTS, D_IN), dtype=jnp.float32) * 0.02
        gate_b = jax.random.normal(k_gb, (NUM_EXPERTS,), dtype=jnp.float32) * 0.02
        expert_w = jax.random.normal(k_ew, (NUM_EXPERTS, D_OUT, D_IN), dtype=jnp.float32) * 0.02
        expert_b = jax.random.normal(k_eb, (NUM_EXPERTS, D_OUT), dtype=jnp.float32) * 0.02
        return {'x': x, 'gate_w': gate_w, 'gate_b': gate_b, 'expert_w': expert_w, 'expert_b': expert_b}
    _L0_ffn_in = _L0_ffn_setup()
    _d = {'L0_attn_hidden_states': _L0_attn_in['hidden_states'], 'L0_attn_W_in': _L0_attn_in['W_in'], 'L0_attn_conv_w': _L0_attn_in['conv_w'], 'L0_attn_conv_b': _L0_attn_in['conv_b'], 'L0_attn_Wx': _L0_attn_in['Wx'], 'L0_attn_dt_ln_w': _L0_attn_in['dt_ln_w'], 'L0_attn_b_ln_w': _L0_attn_in['b_ln_w'], 'L0_attn_c_ln_w': _L0_attn_in['c_ln_w'], 'L0_attn_Wdt': _L0_attn_in['Wdt'], 'L0_attn_dt_bias': _L0_attn_in['dt_bias'], 'L0_attn_A': _L0_attn_in['A'], 'L0_attn_D_param': _L0_attn_in['D_param'], 'L0_attn_W_out': _L0_attn_in['W_out'], 'L0_ffn_gate_w': _L0_ffn_in['gate_w'], 'L0_ffn_gate_b': _L0_ffn_in['gate_b'], 'L0_ffn_expert_w': _L0_ffn_in['expert_w'], 'L0_ffn_expert_b': _L0_ffn_in['expert_b']}
    _x0 = _d['L0_attn_hidden_states']
    _d['L0_attn_hidden_states'] = jax.random.normal(jax.random.fold_in(jax.random.key(seed), 1), (4, 256, 512), dtype=_x0.dtype)
    del _x0
    return _d

def reference(L0_attn_hidden_states, L0_attn_W_in, L0_attn_conv_w, L0_attn_conv_b, L0_attn_Wx, L0_attn_dt_ln_w, L0_attn_b_ln_w, L0_attn_c_ln_w, L0_attn_Wdt, L0_attn_dt_bias, L0_attn_A, L0_attn_D_param, L0_attn_W_out, L0_ffn_gate_w, L0_ffn_gate_b, L0_ffn_expert_w, L0_ffn_expert_b):

    def _L0_attn_ref(hidden_states, W_in, conv_w, conv_b, Wx, dt_ln_w, b_ln_w, c_ln_w, Wdt, dt_bias, A, D_param, W_out):
        import jax, jax.numpy as jnp
        import numpy as np
        H = 512
        D = 1024
        N = 16
        K = 4
        R = 32
        BATCH = 1
        L = 256
        EPS = 1e-06

        def _rmsnorm(x, w):
            return x * jax.lax.rsqrt(jnp.mean(x * x, axis=-1, keepdims=True) + EPS) * w
        proj = hidden_states @ W_in.T
        u, gate = jnp.split(proj, 2, axis=-1)
        x = jnp.transpose(u, (0, 2, 1))
        x = jax.lax.conv_general_dilated(x, conv_w[:, None, :], window_strides=(1,), padding=[(K - 1, 0)], dimension_numbers=('NCH', 'OIH', 'NCH'), feature_group_count=D)
        u = jax.nn.silu(jnp.transpose(x, (0, 2, 1)) + conv_b)
        ssm_p = u @ Wx.T
        dt, Bm, Cm = jnp.split(ssm_p, [R, R + N], axis=-1)
        dt = _rmsnorm(dt, dt_ln_w)
        Bm = _rmsnorm(Bm, b_ln_w)
        Cm = _rmsnorm(Cm, c_ln_w)
        delta = jax.nn.softplus(dt @ Wdt.T + dt_bias)

        def step(state, xs):
            d_t, B_t, C_t, u_t = xs
            dA = jnp.exp(d_t[..., None] * A)
            state = dA * state + (d_t * u_t)[..., None] * B_t[:, None, :]
            y_t = jnp.einsum('bdn,bn->bd', state, C_t)
            return (state, y_t)
        init = jnp.zeros((hidden_states.shape[0], D, N), hidden_states.dtype)
        xs = (jnp.swapaxes(delta, 0, 1), jnp.swapaxes(Bm, 0, 1), jnp.swapaxes(Cm, 0, 1), jnp.swapaxes(u, 0, 1))
        _, ys = jax.lax.scan(step, init, xs)
        y = jnp.swapaxes(ys, 0, 1) + u * D_param
        y = y * jax.nn.silu(gate)
        return y @ W_out.T

    def _L0_ffn_ref(x, gate_w, gate_b, expert_w, expert_b):
        import jax, jax.numpy as jnp
        import numpy as np
        NUM_EXPERTS = 8
        D_IN = 512
        D_OUT = 512
        orig_shape = x.shape
        xf = x.reshape(-1, x.shape[-1])
        gate_logits = xf @ gate_w.T + gate_b
        gates = jax.nn.softmax(gate_logits, axis=-1)
        selected = jnp.argmax(gates, axis=-1)
        out = jnp.zeros((xf.shape[0], expert_w.shape[1]), dtype=xf.dtype)
        for j in range(expert_w.shape[0]):
            yj = xf @ expert_w[j].T + expert_b[j]
            out = out + jnp.where((selected == j)[:, None], yj, 0.0)
        return out.reshape(*orig_shape[:-1], expert_w.shape[1])
    x = L0_attn_hidden_states
    xn = _layernorm(x, axis=-1)
    s = _L0_attn_ref(xn, L0_attn_W_in, L0_attn_conv_w, L0_attn_conv_b, L0_attn_Wx, L0_attn_dt_ln_w, L0_attn_b_ln_w, L0_attn_c_ln_w, L0_attn_Wdt, L0_attn_dt_bias, L0_attn_A, L0_attn_D_param, L0_attn_W_out)
    g = _silu(_L0_ffn_ref(xn, L0_ffn_gate_w, L0_ffn_gate_b, L0_ffn_expert_w, L0_ffn_expert_b))
    x = x + s * g
    return x

_drawn_inputs = setup_inputs


def setup_inputs(seed=0):
    import zlib

    import numpy as np

    out = dict(_drawn_inputs(seed))
    spreads = {'L0_attn_dt_ln_w': (1.0, 0.6),
     'L0_attn_b_ln_w': (1.0, 0.6),
     'L0_attn_c_ln_w': (1.0, 0.6),
     'L0_attn_D_param': (1.0, 0.6)}
    factors = {'L0_attn_W_in': 8.0,
     'L0_attn_conv_w': 8.0,
     'L0_attn_conv_b': 8.0,
     'L0_attn_Wx': 8.0,
     'L0_attn_Wdt': 8.0,
     'L0_attn_dt_bias': 8.0,
     'L0_attn_A': 8.0,
     'L0_attn_W_out': 8.0,
     'L0_ffn_gate_w': 8.0,
     'L0_ffn_gate_b': 8.0,
     'L0_ffn_expert_w': 8.0,
     'L0_ffn_expert_b': 8.0}
    for name, (base, spread) in spreads.items():
        noise = np.random.default_rng([zlib.crc32(name.encode()), seed]).standard_normal(out[name].shape)
        drawn = base * np.exp(spread * noise) if base else spread * noise
        out[name] = jnp.asarray(drawn.astype(out[name].dtype))
    for name, factor in factors.items():
        out[name] = (out[name] * factor).astype(out[name].dtype)
    return out
```

```python
import concourse.bass as bass
from concourse import mybir
from contextlib import ExitStack

F32 = mybir.dt.float32
U32 = mybir.dt.uint32
ALU = mybir.AluOpType
ACT = mybir.ActivationFunctionType
AX = mybir.AxisListType

P = 128
BATCHES, STEPS, HID = 4, 256, 512
CHAN, STATES, TAPS, RANK = 1024, 16, 4, 32
SSM = RANK + 2 * STATES
EXPERTS = 8
TOKENS = BATCHES * STEPS
TT = TOKENS // P
TB = STEPS // P
KT = HID // P
JT = CHAN // P
UNITS = BATCHES * JT
NC = 4
CH = STATES // NC
CW = NC * STEPS
CHUNKS = UNITS * CH
GJ = 8
GW = TB * CHAN // GJ
ETILES = TT + EXPERTS - 1
SLOTS = ETILES * P
LN_EPS, RMS_EPS = 1e-5, 1e-6
SP_CAP = 40.0

R_STATE, R_U, R_DELTA, R_YD = 5, 12, 3, 16

C_ID, C_TRI, C_ONE = 0, P, 2 * P
C_IOTA = 3 * P
C_IOTA8 = C_IOTA + EXPERTS
C_STEP = C_IOTA8 + EXPERTS
C_TILE = C_STEP + EXPERTS
C_MASK = C_TILE + ETILES
C_ALL = C_MASK + EXPERTS * TT
V_TAP, V_CB, V_DTB, V_D, V_A = 0, TAPS, TAPS + 1, TAPS + 2, TAPS + 3
V_ALL = V_A + STATES
ROW_ALL = SSM + EXPERTS


def tasks_at(q):
    t = []
    if q == -1:
        t += [("LN", 0), ("LN", 1), ("T", 0), ("T", 1)]
        t += [(n, j) for j in range(JT) for n in (("U", "SU"))]
        t += [("X", 0, 0), ("X", 0, 1), ("LN", 2), ("N", 0, 0), ("N", 0, 1), ("T", 2), ("D1", 0), ("LN", 3),
              ("D2", 0), ("T", 3), ("D1", 1), ("D2", 1)]
        return t
    i, c = divmod(q, CH)
    if c == 3 and 2 <= i + 2 < UNITS:
        t += [("D2", i + 2)]
    if c == 1 and 1 <= i <= UNITS:
        t += [("Y", i - 1)]
    if c == 2 and 1 <= i <= UNITS:
        t += [("B", i - 1)]
    if 0 <= q < 4:
        t += [("G", 0, 2 * q), ("G", 0, 2 * q + 1)]
    b, r = divmod(q, CH * JT)
    if b + 1 < BATCHES:
        if r % 2 == 0 and r < 2 * JT:
            t += [("U", (b + 1) * JT + r // 2)]
        if r % 2 == 1 and r < 2 * GJ:
            t += [("G", b + 1, r // 2)]
        if r == 17:
            t += [("SU", (b + 1) * JT + j) for j in range(JT)] + [("SG", b + 1)]
        if r in (20, 21):
            t += [("X", b + 1, r - 20)]
        if r in (22, 23):
            t += [("N", b + 1, r - 22)]
    if q == 4:
        t += [("SG", 0)]
    if 1 <= q <= 4:
        t += [("LN", 3 + q), ("T", 3 + q)]
    if q == 5:
        t += [("LOG",), ("RT",)]
    k, r3 = divmod(q - 9, 3)
    if 0 <= k < ETILES:
        t += [("XT", k)] if r3 == 0 else [("E", k)] if r3 == 1 else []
    for ob, gather, silu, first in ((0, 53, 55, 56), (1, 64, 81, 82), (2, 90, 97, 98), (3, 106, 113, CHUNKS + 3)):
        if q == gather:
            t += [("FG", ob)]
        if q == silu:
            t += [("SF", ob)]
        if first <= q < first + 8 and (q - first) % 2 == 0 and ob < 3:
            n = (q - first) // 2
            t += [("O", ob, n // 2, n % 2)]
        if q == first and ob == 3:
            t += [("O", ob, n // 2, n % 2) for n in range(4)]
    if c == 2 and 2 <= i + 2 < UNITS:
        t += [("D1", i + 2)]
    return t


LAST = CHUNKS + 3
PLAN = [(q, tasks_at(q)) for q in range(-1, LAST + 1)]
ORDER = [t for _, ts in PLAN for t in ts]
JOBS = [t for t in ORDER if t[0] in ("T", "U", "X", "N", "D1", "G", "LOG", "RT", "XT", "E", "B", "O")]
JOB = {t: n for n, t in enumerate(JOBS)}


def ordinal(task):
    return [t for t in ORDER if t[0] == task[0]].index(task)


def ssm_moe_program(nc, x, w_u, w_g, chan, w_x, w_dt, rows, gate_w, exp_w, exp_b, w_out, consts, out):
    xs = nc.dram_tensor("tokens_by_expert", (SLOTS, HID), F32, kind="Internal").ap()
    ys = nc.dram_tensor("expert_rows", (SLOTS, HID), F32, kind="Internal").ap()
    bc = nc.dram_tensor("bc_by_state", (BATCHES, 2 * STATES * STEPS), F32, kind="Internal").ap()

    ctx = ExitStack()
    with ctx:
        def sb(name, shape, dt=F32):
            return ctx.enter_context(nc.sbuf_tensor(name, shape, dt))

        def pb(name, shape):
            return ctx.enter_context(nc.psum_tensor(name, shape, F32))

        def sem(name):
            return ctx.enter_context(nc.semaphore(name))

        cst = sb("cst", [P, C_ALL])
        ident = cst[:, C_ID:C_ID + P]
        ch = sb("ch", [P, JT, V_ALL])
        rw = sb("rw", [P, ROW_ALL])
        wu = sb("wu", [P, JT, KT, P])
        wg = sb("wg", [P, KT, CHAN])
        wx = sb("wx", [P, JT, SSM])
        wdt = sb("wdt", [RANK, CHAN])
        gw = sb("gw", [P, KT, EXPERTS])
        shared = sb("shared", [P, TT * HID])
        xn = shared[:, :].rearrange("p (t h) -> p t h", t=TT)
        ew = shared[:, :].rearrange("p (s k h) -> p s k h", s=2, k=KT)
        wo = shared[:, :].rearrange("p (j h) -> p j h", j=JT)
        xnt = sb("xnt", [P, KT, TOKENS])
        ur = sb("ur", [P, R_U, STEPS])
        dl = sb("dl", [P, R_DELTA, STEPS])
        spx = sb("spx", [P, 2, STEPS])
        ud = sb("ud", [P, 2, STEPS])
        st = sb("st", [P, R_STATE, CW])
        bb = sb("bb", [P, STATES * STEPS])
        cb = sb("cb", [P, STATES * STEPS])
        gt = sb("gt", [P, 2, TB, CHAN])
        ygt = sb("ygt", [P, 2, TB, P])
        yd = sb("yd", [P, R_YD, STEPS])
        xg = sb("xg", [P, 2, HID])
        xgt = sb("xgt", [P, KT, P])
        ebr = sb("ebr", [P, 2, HID])
        yr = sb("yr", [P, 2, HID])
        fg = sb("fg", [P, TB, HID])
        xr = sb("xr", [P, TB, HID])
        stats = sb("stats", [P, TT, 6])
        mv = sb("mv", [P, TT, 2])
        rstd = sb("rstd", [P, TT])
        half = sb("half", [P, 4])
        ssm = sb("ssm", [P, 2, SSM])
        sq = sb("sq", [P, SSM])
        ms = sb("ms", [P, 2, 4])
        rms = sb("rms", [P, 2, 4])
        nrm = sb("nrm", [P, 2, SSM])
        nt = sb("nt", [SSM, 2, STEPS])
        NE = EXPERTS * TT
        lg = sb("lg", [P, NE])
        eq = sb("eq", [P, NE])
        oneh = sb("oneh", [P, NE])
        cnt = sb("cnt", [P, 2 * NE])
        tot = sb("tot", [P, NE])
        inc = sb("inc", [P, NE])
        s8 = sb("s8", [P, 8, EXPERTS])
        big = sb("bigcmp", [P, ETILES * EXPERTS])
        slot = sb("slot", [P, TT], U32)
        ek = sb("ek", [P, ETILES], U32)

        dA = [pb(f"dA{s}", [P, CW]) for s in range(2)]
        wp = pb("wp", [P, 2, STEPS])
        yp = pb("yp", [P, 2 * STEPS])
        mp = [pb(f"mp{s}", [P, 2 * STEPS]) for s in range(2)]
        ysum = yp[:, 0:TB * P].rearrange("p (t c) -> p t c", t=TB)

        l_x = [sem(f"l_x{t}") for t in range(TT)]
        l_wu = [sem(f"l_wu{j}") for j in range(JT)]
        l_cst, l_ch, l_rw, l_wx, l_wdt, l_gw, l_wg, l_wo = (sem(n) for n in (
            "l_cst", "l_ch", "l_rw", "l_wx", "l_wdt", "l_gw", "l_wg", "l_wo"))
        l_b = [sem(f"l_b{c}") for c in range(CH)]
        l_c = [sem(f"l_c{c}") for c in range(CH)]
        l_e = [sem(f"l_e{s}") for s in range(2)]
        l_xr = [sem(f"l_xr{t}") for t in range(TB)]
        l_fg = [sem(f"l_fg{t}") for t in range(TB)]
        s_zero, s_bc, s_scat = sem("s_zero"), sem("s_bc"), sem("s_scat")
        s_ys = [sem(f"s_ys{s}") for s in range(2)]
        s_out = [sem(f"s_out{t}") for t in range(TB)]
        exp_done, wb_done, scan_done, cm_done, nsum_done = (sem(n) for n in (
            "exp_done", "wb_done", "scan_done", "cm_done", "nsum_done"))
        filled = {n: sem(f"filled_{n}") for n in ("T", "U", "X", "N", "D1", "G", "LOG", "RT", "XT", "E", "B", "O")}
        freed = {n: sem(f"freed_{n}") for n in filled}
        cleared, zeroed, const_half = sem("cleared"), sem("zeroed"), sem("const_half")
        var_done, rstd_done, xn_done = sem("var_done"), sem("rstd_done"), sem("xn_done")
        silu_u, silu_g, silu_f, ud_done = sem("silu_u"), sem("silu_g"), sem("silu_f"), sem("ud_done")
        ms_done, rms_done, nrm_done = sem("ms_done"), sem("rms_done"), sem("nrm_done")
        spx_done, spe_done, spl_done, w_done = sem("spx_done"), sem("spe_done"), sem("spl_done"), sem("w_done")
        y_taken = sem("y_taken")
        oneh_done, routed = sem("oneh_done"), sem("routed")
        out_done, chain = sem("out_done"), sem("chain")

        block = ctx.enter_context(nc.Block())

        def state(q):
            return st[:, q % R_STATE, :].rearrange("p (n t) -> p n t", n=NC)

        def bank(task):
            return mp[JOB[task] % 2]

        @block.sync
        def _(sp):
            def x_tile(t):
                return x[t * P:(t + 1) * P, :]

            for t in range(2):
                sp.dma_start(xn[:, t, :], x_tile(t)).then_inc(l_x[t], 16)
            for j in range(JT):
                sp.dma_start(wu[:, j, :, :], w_u[:, j, :, :]).then_inc(l_wu[j], 16)
            for t in range(2, TT):
                sp.dma_start(xn[:, t, :], x_tile(t)).then_inc(l_x[t], 16)
            sp.dma_start(wg[:, :, :], w_g).then_inc(l_wg, 16)

            def store_bc(b):
                sp.wait_ge(freed["N"], TB * (b + 1))
                sp.dma_start(bc[b].rearrange("(s t) -> s t", t=STEPS), nt[RANK:SSM, b % 2, :]).then_inc(s_bc, 16)

            def load_bc(b, c, which):
                sp.wait_ge(s_bc, 16 * (b + 1))
                last = CH * JT * b - CH + c
                if which == 0:
                    if b:
                        sp.wait_ge(wb_done, last + 1)
                    src = bc[b, c * CW:(c + 1) * CW]
                    sp.dma_start(bb[:, c * CW:(c + 1) * CW], src.partition_broadcast(P)).then_inc(l_b[c], 16)
                else:
                    if b:
                        sp.wait_ge(cm_done, last + 1)
                    src = bc[b, (CH + c) * CW:(CH + c + 1) * CW]
                    sp.dma_start(cb[:, c * CW:(c + 1) * CW], src.partition_broadcast(P)).then_inc(l_c[c], 16)

            def load_expert_tile(k):
                s = k % 2
                if k == 0:
                    sp.wait_ge(s_scat, 16 * TT)
                    sp.wait_ge(freed["T"], TT)
                if k >= 2:
                    sp.wait_ge(filled["E"], k - 1)
                    sp.wait_ge(freed["E"], k - 1)
                e = sp.value_load(ek[0:1, k:k + 1], min_val=0, max_val=EXPERTS - 1)
                sp.dma_start(xg[:, s, :], xs[k * P:(k + 1) * P, :]).then_inc(l_e[s], 16)
                sp.dma_start(ew[:, s, :, :], exp_w[bass.ds(e, 1), :, :, :].rearrange("o p k h -> (o p) k h")).then_inc(l_e[s], 16)
                sp.dma_start(ebr[:, s, :], exp_b[bass.ds(e, 1), :].broadcast_to([P, HID])).then_inc(l_e[s], 16)

            def store_expert_tile(k):
                sp.wait_ge(freed["E"], k + 1)
                sp.dma_start(ys[k * P:(k + 1) * P, :], yr[:, k % 2, :]).then_inc(s_ys[k % 2], 16)

            def load_residual(b, tt):
                if b:
                    sp.wait_ge(s_out[tt], 16 * b)
                else:
                    sp.wait_ge(s_zero, 16)
                sp.dma_start(xr[:, tt, :], x_tile(TB * b + tt)).then_inc(l_xr[tt], 16)

            store_bc(0)
            for c in range(CH):
                load_bc(0, c, 0)
            for c in range(CH):
                load_bc(0, c, 1)
            for q, tasks in PLAN[1:]:
                b, r = divmod(q, CH * JT)
                if b + 1 < BATCHES and r == 24:
                    store_bc(b + 1)
                if b + 1 < BATCHES and r >= 28:
                    load_bc(b + 1, r - 28, 0)
                if 1 <= b < BATCHES and r < CH:
                    load_bc(b, r, 1)
                if q == 6:
                    sp.wait_ge(routed, 1)
                k, r3 = divmod(q - 6, 3)
                if k in (0,) and r3 == 0:
                    load_expert_tile(0)
                if r3 == 0 and 0 <= k and k + 1 < ETILES:
                    load_expert_tile(k + 1)
                for t in tasks:
                    if t[0] == "E":
                        store_expert_tile(t[1])
                    if t == ("E", ETILES - 1):
                        sp.wait_ge(filled["E"], ETILES)
                        sp.dma_start(wo, w_out).then_inc(l_wo, 16)
                        load_residual(0, 0)
                        load_residual(0, 1)
                    if t[0] == "O" and t[3] == 1:
                        _, ob, tt, _ = t
                        sp.wait_ge(out_done, ordinal(t) + 1)
                        row = (TB * ob + tt) * P
                        sp.dma_start(out[row:row + P, :], xr[:, tt, :]).then_inc(s_out[tt], 16)
                        if ob + 1 < BATCHES:
                            load_residual(ob + 1, tt)
            for tt in range(TB):
                sp.wait_ge(s_out[tt], 16 * BATCHES)

        @block.gpsimd
        def _(pool):
            pool.memset(half[:, :], -0.5).then_inc(const_half, 1)
            pool.wait_ge(zeroed, 1)
            pool.dma_start(xs.rearrange("(k p) h -> p k h", p=P),
                           xr[:, 0:1, :].broadcast_to([P, ETILES, HID])).then_inc(s_zero, 16)
            pool.wait_ge(const_half, 1)
            for q, tasks in PLAN:
                if 0 <= q < CHUNKS:
                    i, c = divmod(q, CH)
                    pool.wait_ge(l_c[c], 16 * (i // JT + 1))
                    pool.wait_ge(scan_done, q + 1)
                    nc.gpsimd.tensor_tensor(st[:, q % R_STATE, :], st[:, q % R_STATE, :], cb[:, c * CW:(c + 1) * CW],
                                            ALU.mult).then_inc(cm_done, 1)
                for t in tasks:
                    if t[0] == "LN":
                        pool.wait_ge(var_done, t[1] + 1)
                        nc.gpsimd.tensor_tensor(rstd[:, t[1]:t[1] + 1], mv[:, t[1], 1:2], half[:, 0:1],
                                                ALU.pow).then_inc(rstd_done, 1)
                    if t[0] == "X":
                        n = ordinal(t)
                        pool.wait_ge(ms_done, n + 1)
                        if n >= 2:
                            pool.wait_ge(nrm_done, n - 1)
                        nc.gpsimd.tensor_tensor(rms[:, n % 2, 0:3], ms[:, n % 2, 0:3], half[:, 0:3],
                                                ALU.pow).then_inc(rms_done, 1)
                    if t[0] == "RT":
                        pool.wait_ge(routed, 1)
                        pool.wait_ge(s_zero, 16)
                        pool.wait_ge(xn_done, TT)
                        for tt in range(TT):
                            pool.indirect_dma_start(xs, bass.IndirectOffsetOnAxis(ap=slot[:, tt:tt + 1], axis=0),
                                                    xn[:, tt, :], None).then_inc(s_scat, 16)
                    if t[0] == "FG":
                        b = t[1]
                        if b == 0:
                            pool.wait_ge(s_ys[0], 16 * ((ETILES + 1) // 2))
                            pool.wait_ge(s_ys[1], 16 * (ETILES // 2))
                        else:
                            pool.wait_ge(out_done, 2 * TB * b)
                        for tt in range(TB):
                            tile = TB * b + tt
                            pool.indirect_dma_start(fg[:, tt, :], None, ys,
                                                    bass.IndirectOffsetOnAxis(ap=slot[:, tile:tile + 1], axis=0)
                                                    ).then_inc(l_fg[tt], 16)

        @block.scalar
        def _(act):
            act.dma_start(cst[:, :], consts).then_inc(l_cst, 16)
            act.dma_start(ch[:, :, :], chan).then_inc(l_ch, 16)
            act.dma_start(rw[:, :], rows.broadcast_to([P, ROW_ALL])).then_inc(l_rw, 16)
            act.dma_start(wx[:, :, :], w_x).then_inc(l_wx, 16)
            act.dma_start(wdt[:, :], w_dt).then_inc(l_wdt, 16)
            act.dma_start(gw[:, :, :], gate_w).then_inc(l_gw, 16)
            nc.scalar.preload_act_table_set("silu_and_others")
            act.wait_ge(l_ch, 16)

            def exps(q):
                i, c = divmod(q, CH)
                j = i % JT
                if q == 0:
                    act.wait_ge(cleared, 1)
                if c == 0:
                    act.wait_ge(freed["D1"], i + 1)
                if q >= 2:
                    act.wait_ge(scan_done, q - 1)
                for n in range(NC):
                    at = V_A + NC * c + n
                    last = nc.scalar.activation(dA[q % 2][:, n * STEPS + 1:(n + 1) * STEPS], dl[:, i % R_DELTA, 1:STEPS],
                                                ACT.Exp, scale=ch[:, j, at:at + 1])
                last.then_inc(exp_done, 1)

            def skip(i):
                act.wait_ge(silu_u, i + 1)
                if i >= 2:
                    act.wait_ge(nsum_done, CH * (i - 2) + 1)
                j = i % JT
                nc.scalar.activation(ud[:, i % 2, :], ur[:, i % R_U, :], ACT.Copy,
                                     scale=ch[:, j, V_D:V_D + 1]).then_inc(ud_done, 1)

            def table(name):
                nc.scalar.preload_act_table_set(name)

            silus = ("SU", "SG", "SF")
            for q, tasks in PLAN:
                if 0 <= q < CHUNKS:
                    exps(q)
                    if q % CH == 0:
                        skip(q // CH)
                for at, t in enumerate(tasks):
                    n = ordinal(t)
                    if q >= 0 and t[0] in silus and (not at or tasks[at - 1][0] not in silus):
                        table("silu_and_others")
                    if t[0] in ("T", "N", "G", "XT", "B"):
                        act.wait_ge(filled[t[0]], n + 1)
                        m = bank(t)
                    if t[0] == "T":
                        nc.scalar.activation(xnt[:, :, t[1] * P:(t[1] + 1) * P],
                                             m[:, 0:KT * P].rearrange("p (k c) -> p k c", k=KT), ACT.Copy
                                             ).then_inc(freed["T"], 1)
                    if t[0] == "N":
                        _, b, tt = t
                        if b >= 2:
                            act.wait_ge(filled["D1"], JT * (b - 1))
                            act.wait_ge(s_bc, 16 * (b - 1))
                        nc.scalar.activation(nt[:, b % 2, tt * P:(tt + 1) * P], m[0:SSM, 0:P],
                                             ACT.Copy).then_inc(freed["N"], 1)
                    if t[0] == "G":
                        _, b, g = t
                        if b >= 2:
                            act.wait_ge(y_taken, JT * (b - 1))
                        tt, col = divmod(g * GW, CHAN)
                        nc.scalar.activation(gt[:, b % 2, tt, col:col + GW], m[:, 0:GW],
                                             ACT.Copy).then_inc(freed["G"], 1)
                    if t[0] == "XT":
                        if n:
                            act.wait_ge(filled["E"], n)
                        nc.scalar.activation(xgt[:, :, :], m[:, 0:KT * P].rearrange("p (k c) -> p k c", k=KT),
                                             ACT.Copy).then_inc(freed["XT"], 1)
                    if t[0] == "B":
                        i = t[1]
                        if i >= R_YD:
                            act.wait_ge(filled["O"], 2 * TB * (i // JT - 1))
                        nc.scalar.activation(yd[:, i % R_YD, :], m[:, 0:STEPS], ACT.Copy).then_inc(freed["B"], 1)
                    if t[0] == "SU":
                        act.wait_ge(freed["U"], t[1] + 1)
                        nc.scalar.activation(ur[:, t[1] % R_U, :], ur[:, t[1] % R_U, :], ACT.Silu).then_inc(silu_u, 1)
                    if t[0] == "SG":
                        b = t[1]
                        act.wait_ge(freed["G"], GJ * (b + 1))
                        for tt in range(TB):
                            nc.scalar.activation(gt[:, b % 2, tt, :], gt[:, b % 2, tt, :], ACT.Silu).then_inc(silu_g, 1)
                    if t[0] == "SF":
                        for tt in range(TB):
                            act.wait_ge(l_fg[tt], 16 * (t[1] + 1))
                            nc.scalar.activation(fg[:, tt, :], fg[:, tt, :], ACT.Silu).then_inc(silu_f, 1)
                    after = tasks[at + 1][0] if at + 1 < len(tasks) else None
                    if q >= 0 and t[0] in silus and after not in silus or t == ("SU", JT - 1):
                        table("natural_log_exp_and_others")
                    if t[0] == "D1":
                        i = t[1]
                        act.wait_ge(spx_done, i + 1)
                        nc.scalar.activation(spx[:, i % 2, :], spx[:, i % 2, :], ACT.Exp).then_inc(spe_done, 1)
                        act.wait_ge(spe_done, i + 1)
                        nc.scalar.activation(spx[:, i % 2, :], spx[:, i % 2, :], ACT.Ln, bias=1.0).then_inc(spl_done, 1)

        @block.vector
        def _(dve):
            links = [0]

            def link(ins):
                links[0] += 1
                ins.then_inc(chain, 1)
                dve.wait_ge(chain, links[0])

            nc.vector.memset(xr[:, 0, :], 0.0).then_inc(zeroed, 1)
            for s in range(2):
                last = nc.vector.memset(dA[s][:, 0:CW].rearrange("p (n t) -> p n t", n=NC)[:, :, 0:1], 0.0)
            last.then_inc(cleared, 1)

            def product(q):
                i, c = divmod(q, CH)
                dve.wait_ge(l_b[c], 16 * (i // JT + 1))
                dve.wait_ge(w_done, i + 1)
                if q >= R_STATE:
                    dve.wait_ge(nsum_done, q - R_STATE + 1)
                nc.vector.tensor_tensor(state(q), wp[:, i % 2, :].unsqueeze(1).broadcast_to([P, NC, STEPS]),
                                        bb[:, c * CW:(c + 1) * CW].rearrange("p (n t) -> p n t", n=NC),
                                        ALU.mult).then_inc(wb_done, 1)

            def scan(q):
                dve.wait_ge(exp_done, q + 1)
                dve.wait_ge(wb_done, q + 1)
                nc.vector.tensor_tensor_scan(st[:, q % R_STATE, :], dA[q % 2][:, :], st[:, q % R_STATE, :], 0.0,
                                             ALU.mult, ALU.add).then_inc(scan_done, 1)

            def layernorm(t):
                dve.wait_ge(l_x[t], 16)
                link(nc.vector.bn_stats(stats[:, t, :], xn[:, t, :]))
                link(nc.vector.bn_aggr(mv[:, t, :], stats[:, t, :]))
                nc.vector.tensor_scalar(mv[:, t, 1:2], mv[:, t, 1:2], LN_EPS, None, ALU.add).then_inc(var_done, 1)
                dve.wait_ge(rstd_done, t + 1)
                nc.vector.tensor_scalar(xn[:, t, :], xn[:, t, :], mv[:, t, 0:1], rstd[:, t:t + 1],
                                        ALU.subtract, ALU.mult).then_inc(xn_done, 1)

            def conv(i, m):
                j = i % JT
                if i >= R_U:
                    dve.wait_ge(ud_done, i - R_U + 1)
                    dve.wait_ge(filled["X"], TB * ((i - R_U) // JT + 1))
                o = ur[:, i % R_U, :]
                link(nc.vector.tensor_scalar(o, m[:, 0:STEPS], ch[:, j, TAPS - 1:TAPS], ch[:, j, V_CB:V_CB + 1],
                                             ALU.mult, ALU.add))
                for k in range(1, TAPS):
                    tap = ch[:, j, TAPS - 1 - k:TAPS - k]
                    ins = nc.vector.scalar_tensor_tensor(out=o[:, k:STEPS], in0=m[:, 0:STEPS - k], scalar=tap,
                                                         in1=o[:, k:STEPS], op0=ALU.mult, op1=ALU.add)
                    if k < TAPS - 1:
                        link(ins)
                ins.then_inc(freed["U"], 1)

            def squares(n, m):
                s = ssm[:, n % 2, :]
                if n >= 2:
                    dve.wait_ge(rms_done, n - 1)
                    dve.wait_ge(nrm_done, n - 1)
                nc.vector.tensor_copy(s, m[:, 0:SSM]).then_inc(freed["X"], 1)
                dve.wait_ge(freed["X"], n + 1)
                link(nc.vector.tensor_tensor(sq[:, :], s, s, ALU.mult))
                nc.vector.tensor_reduce(ms[:, n % 2, 0:1], sq[:, 0:RANK], AX.X, ALU.add)
                link(nc.vector.tensor_reduce(ms[:, n % 2, 1:3], sq[:, RANK:SSM].rearrange("p (a s) -> p a s", a=2),
                                             AX.X, ALU.add))
                nc.vector.tensor_scalar(ms[:, n % 2, 0:1], ms[:, n % 2, 0:1], 1.0 / RANK, RMS_EPS, ALU.mult, ALU.add)
                nc.vector.tensor_scalar(ms[:, n % 2, 1:3], ms[:, n % 2, 1:3], 1.0 / STATES, RMS_EPS,
                                        ALU.mult, ALU.add).then_inc(ms_done, 1)

            def rmsnorm(n):
                dve.wait_ge(rms_done, n + 1)
                if n >= 2:
                    dve.wait_ge(filled["N"], n - 1)
                for part, (a, b) in enumerate(((0, RANK), (RANK, RANK + STATES), (RANK + STATES, SSM))):
                    last = nc.vector.scalar_tensor_tensor(out=nrm[:, n % 2, a:b], in0=ssm[:, n % 2, a:b],
                                                          scalar=rms[:, n % 2, part:part + 1], in1=rw[:, a:b],
                                                          op0=ALU.mult, op1=ALU.mult)
                last.then_inc(nrm_done, 1)

            def choose(m):
                def v(a):
                    return a[:, :].rearrange("p (t e) -> p t e", e=EXPERTS)

                def by_expert(a):
                    return a.unsqueeze(1).broadcast_to([P, TT, EXPERTS])

                def by_tile(a):
                    return a.unsqueeze(2).broadcast_to([P, TT, EXPERTS])
                nc.vector.tensor_tensor(v(lg), m[:, 0:NE].rearrange("p (t e) -> p t e", e=EXPERTS),
                                        by_expert(rw[:, SSM:ROW_ALL]), ALU.add).then_inc(freed["LOG"], 1)
                dve.wait_ge(freed["LOG"], 1)
                link(nc.vector.tensor_reduce(s8[:, 0, :], v(lg), AX.X, ALU.max))
                link(nc.vector.tensor_tensor(v(eq), v(lg), by_tile(s8[:, 0, :]), ALU.is_equal))
                link(nc.vector.scalar_tensor_tensor(out=v(eq), in0=v(eq), scalar=-float(EXPERTS),
                                                    in1=by_expert(cst[:, C_IOTA8:C_IOTA8 + EXPERTS]),
                                                    op0=ALU.mult, op1=ALU.add))
                link(nc.vector.tensor_reduce(s8[:, 1, :], v(eq), AX.X, ALU.min))
                nc.vector.tensor_tensor(v(oneh), by_expert(cst[:, C_IOTA:C_IOTA + EXPERTS]), by_tile(s8[:, 1, :]),
                                        ALU.is_equal).then_inc(oneh_done, 1)

            def route(m):
                nc.vector.tensor_copy(cnt[:, :], m[:, 0:2 * NE]).then_inc(freed["RT"], 1)
                dve.wait_ge(freed["RT"], 1)
                te, et = "p (t e) -> p t e", "p (e t) -> p e t"
                link(nc.vector.tensor_copy(tot[:, :].rearrange(et, e=EXPERTS),
                                           cnt[:, NE:2 * NE].rearrange("p (t e) -> p e t", e=EXPERTS)))
                link(nc.vector.tensor_tensor_scan(inc[:, :], cst[:, C_MASK:C_MASK + NE], tot[:, :], 0.0,
                                                  ALU.mult, ALU.add))
                link(nc.vector.tensor_tensor(tot[:, :], inc[:, :], tot[:, :], ALU.subtract))
                count = inc[:, :].rearrange(et, e=EXPERTS)[:, :, TT - 1:TT].broadcast_to([P, EXPERTS, TT])
                steps = cst[:, C_STEP:C_STEP + TT].unsqueeze(1).broadcast_to([P, EXPERTS, TT])
                link(nc.vector.tensor_tensor(eq[:, :].rearrange(et, e=EXPERTS), count, steps, ALU.is_gt))
                link(nc.vector.tensor_reduce(s8[:, 2, :], eq[:, :].rearrange(et, e=EXPERTS), AX.X, ALU.add))
                link(nc.vector.tensor_tensor_scan(s8[:, 3, :], cst[:, C_ONE:C_ONE + EXPERTS], s8[:, 2, :], 0.0,
                                                  ALU.mult, ALU.add))
                link(nc.vector.tensor_tensor(s8[:, 4, :], s8[:, 3, :], s8[:, 2, :], ALU.subtract))
                link(nc.vector.tensor_scalar(s8[:, 4, :], s8[:, 4, :], float(P), None, ALU.mult))
                rank = eq[:, :].rearrange(te, e=EXPERTS)
                link(nc.vector.tensor_tensor(rank, cnt[:, 0:NE].rearrange(te, e=EXPERTS),
                                             tot[:, :].rearrange("p (e t) -> p t e", e=EXPERTS), ALU.add))
                link(nc.vector.tensor_tensor(rank, rank, s8[:, 4, :].unsqueeze(1).broadcast_to([P, TT, EXPERTS]), ALU.add))
                link(nc.vector.tensor_tensor(eq[:, :], eq[:, :], oneh[:, :], ALU.mult))
                link(nc.vector.tensor_reduce(s8[:, 5, :], rank, AX.X, ALU.add))
                link(nc.vector.tensor_copy(slot[:, :], s8[:, 5, :]))
                cmp = big[:, :].rearrange("p (k e) -> p k e", e=EXPERTS)
                link(nc.vector.tensor_tensor(cmp, s8[:, 3, :].unsqueeze(1).broadcast_to([P, ETILES, EXPERTS]),
                                             cst[:, C_TILE:C_TILE + ETILES].unsqueeze(2).broadcast_to([P, ETILES, EXPERTS]),
                                             ALU.is_le))
                link(nc.vector.tensor_reduce(lg[:, 0:ETILES], cmp, AX.X, ALU.add))
                nc.vector.tensor_scalar(ek[:, :], lg[:, 0:ETILES], float(EXPERTS - 1), None, ALU.min).then_inc(routed, 1)

            def softplus_in(i, m):
                if i >= 2:
                    dve.wait_ge(freed["D1"], i - 1)
                nc.vector.tensor_scalar(spx[:, i % 2, :], m[:, 0:STEPS], ch[:, i % JT, V_DTB:V_DTB + 1], SP_CAP,
                                        ALU.add, ALU.min).then_inc(spx_done, 1)

            def softplus_out(i, m):
                dve.wait_ge(spl_done, i + 1)
                if i >= R_DELTA:
                    dve.wait_ge(exp_done, CH * (i - R_DELTA + 1))
                nc.vector.scalar_tensor_tensor(out=dl[:, i % R_DELTA, :], in0=m[:, 0:STEPS],
                                               scalar=ch[:, i % JT, V_DTB:V_DTB + 1], in1=spx[:, i % 2, :],
                                               op0=ALU.add, op1=ALU.max).then_inc(freed["D1"], 1)
                dve.wait_ge(freed["D1"], i + 1)
                dve.wait_ge(silu_u, i + 1)
                if i >= 2:
                    dve.wait_ge(wb_done, CH * (i - 1))
                nc.vector.tensor_tensor(wp[:, i % 2, :], dl[:, i % R_DELTA, :], ur[:, i % R_U, :],
                                        ALU.mult).then_inc(w_done, 1)

            for q, tasks in PLAN:
                if 0 <= q < CHUNKS:
                    if q == 0:
                        product(0)
                    if q + 1 < CHUNKS:
                        product(q + 1)
                    scan(q)
                for t in tasks:
                    n = ordinal(t)
                    if t[0] in ("U", "X", "LOG", "RT", "D1", "E", "O"):
                        dve.wait_ge(filled[t[0]], n + 1)
                        m = bank(t)
                    if t[0] == "LN":
                        layernorm(t[1])
                    if t[0] == "U":
                        if n == 0:
                            dve.wait_ge(l_ch, 16)
                        conv(n, m)
                    if t[0] == "X":
                        squares(n, m)
                    if t[0] == "N":
                        if n == 0:
                            dve.wait_ge(l_rw, 16)
                        rmsnorm(n)
                    if t[0] == "LOG":
                        dve.wait_ge(l_cst, 16)
                        choose(m)
                    if t[0] == "RT":
                        route(m)
                    if t[0] == "D1":
                        softplus_in(n, m)
                    if t[0] == "D2":
                        softplus_out(n, bank(("D1", n)))
                    if t[0] == "Y":
                        i = t[1]
                        b, j = divmod(i, JT)
                        dve.wait_ge(nsum_done, CH * (i + 1))
                        dve.wait_ge(silu_g, TB * (b + 1))
                        if i >= 2:
                            dve.wait_ge(filled["B"], i - 1)
                        nc.vector.tensor_tensor(ygt[:, i % 2, :, :], ysum, gt[:, b % 2, :, j * P:(j + 1) * P],
                                                ALU.mult).then_inc(y_taken, 1)
                    if t[0] == "E":
                        if n >= 2:
                            dve.wait_ge(s_ys[n % 2], 16 * (n // 2))
                        nc.vector.tensor_tensor(yr[:, n % 2, :], m[:, 0:HID], ebr[:, n % 2, :],
                                                ALU.add).then_inc(freed["E"], 1)
                    if t[0] == "O":
                        _, b, tt, h = t
                        cols = slice(h * STEPS, (h + 1) * STEPS)
                        dve.wait_ge(silu_f, TB * b + tt + 1)
                        dve.wait_ge(l_xr[tt], 16 * (b + 1))
                        nc.vector.tensor_tensor(fg[:, tt, cols], m[:, 0:STEPS], fg[:, tt, cols],
                                                ALU.mult).then_inc(freed["O"], 1)
                        dve.wait_ge(freed["O"], n + 1)
                        nc.vector.tensor_tensor(xr[:, tt, cols], xr[:, tt, cols], fg[:, tt, cols],
                                                ALU.add).then_inc(out_done, 1)

        @block.tensor
        def _(pe):
            def mm(o, l, r, start, stop):
                return nc.tensor.matmul(o, l, r, start=start, stop=stop, skip_group_check=True)

            def flip(o, src, start=True, stop=True):
                return nc.tensor.matmul(o, src, ident, is_transpose=True, start=start, stop=stop, skip_group_check=True)

            def sum_states(q):
                i, c = divmod(q, CH)
                if c == 0:
                    pe.wait_ge(ud_done, i + 1)
                    if i:
                        pe.wait_ge(y_taken, i)
                    for tt in range(TB):
                        flip(ysum[:, tt, :], ud[:, i % 2, tt * P:(tt + 1) * P], start=(tt == 0), stop=False)
                pe.wait_ge(cm_done, q + 1)
                for n in range(NC):
                    for tt in range(TB):
                        at = n * STEPS + tt * P
                        last = flip(ysum[:, tt, :], st[:, q % R_STATE, at:at + P], start=False,
                                    stop=(c == CH - 1 and n == NC - 1))
                last.then_inc(nsum_done, 1)

            pe.wait_ge(l_cst, 16)
            for q, tasks in PLAN:
                if 0 <= q - 2 < CHUNKS:
                    sum_states(q - 2)
                for t in tasks:
                    if t not in JOB:
                        continue
                    n = ordinal(t)
                    if JOB[t] >= 2:
                        before = JOBS[JOB[t] - 2]
                        pe.wait_ge(freed[before[0]], ordinal(before) + 1)
                    m = bank(t)
                    if t[0] == "T":
                        pe.wait_ge(xn_done, n + 1)
                        for k in range(KT):
                            last = flip(m[:, k * P:(k + 1) * P], xn[:, t[1], k * P:(k + 1) * P])
                    if t[0] == "U":
                        b, j = divmod(t[1], JT)
                        if b == 0:
                            pe.wait_ge(l_wu[j], 16)
                        pe.wait_ge(freed["T"], TB * (b + 1))
                        for k in range(KT):
                            last = mm(m[:, 0:STEPS], wu[:, j, k, :], xnt[:, k, b * STEPS:(b + 1) * STEPS], k == 0, k == KT - 1)
                    if t[0] == "X":
                        _, b, tt = t
                        if n == 0:
                            pe.wait_ge(l_wx, 16)
                        pe.wait_ge(silu_u, JT * (b + 1))
                        for j in range(JT):
                            last = mm(m[:, 0:SSM], ur[:, (JT * b + j) % R_U, tt * P:(tt + 1) * P], wx[:, j, :], j == 0, j == JT - 1)
                    if t[0] == "N":
                        pe.wait_ge(nrm_done, n + 1)
                        last = flip(m[0:SSM, 0:P], nrm[:, n % 2, :])
                    if t[0] == "D1":
                        b, j = divmod(t[1], JT)
                        if n == 0:
                            pe.wait_ge(l_wdt, 16)
                        pe.wait_ge(freed["N"], TB * (b + 1))
                        last = mm(m[:, 0:STEPS], wdt[:, j * P:(j + 1) * P], nt[0:RANK, b % 2, :], True, True)
                    if t[0] == "G":
                        _, b, g = t
                        if n == 0:
                            pe.wait_ge(l_wg, 16)
                        tt, col = divmod(g * GW, CHAN)
                        at = (TB * b + tt) * P
                        pe.wait_ge(freed["T"], TB * (b + 1))
                        for k in range(KT):
                            last = mm(m[:, 0:GW], xnt[:, k, at:at + P], wg[:, k, col:col + GW], k == 0, k == KT - 1)
                    if t[0] == "LOG":
                        pe.wait_ge(l_gw, 16)
                        pe.wait_ge(freed["T"], TT)
                        for tt in range(TT):
                            for k in range(KT):
                                last = mm(m[:, tt * EXPERTS:(tt + 1) * EXPERTS], xnt[:, k, tt * P:(tt + 1) * P], gw[:, k, :],
                                          k == 0, k == KT - 1)
                    if t[0] == "RT":
                        pe.wait_ge(oneh_done, 1)
                        mm(m[:, 0:NE], cst[:, C_TRI:C_TRI + P], oneh[:, :], True, True)
                        last = mm(m[:, NE:2 * NE], cst[:, C_ONE:C_ONE + P], oneh[:, :], True, True)
                    if t[0] == "XT":
                        pe.wait_ge(l_e[n % 2], 48 * (n // 2 + 1))
                        for k in range(KT):
                            last = flip(m[:, k * P:(k + 1) * P], xg[:, n % 2, k * P:(k + 1) * P])
                    if t[0] == "E":
                        pe.wait_ge(freed["XT"], n + 1)
                        for k in range(KT):
                            last = mm(m[:, 0:HID], xgt[:, k, :], ew[:, n % 2, k, :], k == 0, k == KT - 1)
                    if t[0] == "B":
                        pe.wait_ge(y_taken, t[1] + 1)
                        for tt in range(TB):
                            last = flip(m[:, tt * P:(tt + 1) * P], ygt[:, t[1] % 2, tt, :])
                    if t[0] == "O":
                        _, b, tt, h = t
                        if n == 0:
                            pe.wait_ge(l_wo, 16)
                        pe.wait_ge(freed["B"], JT * (b + 1))
                        for j in range(JT):
                            last = mm(m[:, 0:STEPS], yd[:, (JT * b + j) % R_YD, tt * P:(tt + 1) * P],
                                      wo[:, j, h * STEPS:(h + 1) * STEPS], j == 0, j == JT - 1)
                    last.then_inc(filled[t[0]], 1)


def constants():
    import numpy as np
    c = np.zeros((P, C_ALL), np.float32)
    c[:, C_ID:C_ID + P] = np.eye(P)
    c[:, C_TRI:C_TRI + P] = np.triu(np.ones((P, P)), 1)
    c[:, C_ONE:C_ONE + P] = 1
    c[:, C_IOTA:C_IOTA + EXPERTS] = np.arange(EXPERTS)
    c[:, C_IOTA8:C_IOTA8 + EXPERTS] = np.arange(EXPERTS) + EXPERTS
    c[:, C_STEP:C_STEP + TT] = np.arange(TT) * P
    c[:, C_TILE:C_TILE + ETILES] = np.arange(ETILES)
    c[:, C_MASK:C_MASK + EXPERTS * TT] = np.arange(EXPERTS * TT) % TT != 0
    return c


def kernel(**inputs):
    import numpy as np
    import concourse.bacc as bacc
    from concourse.bass_utils import run_bass_kernel_spmd

    i = {k.removeprefix("L0_"): np.asarray(v) for k, v in inputs.items()}

    def tiled(a, tiles):
        return a.reshape(tiles, P, -1).transpose(1, 0, 2)

    w_in = i["attn_W_in"]
    per_channel = np.concatenate(
        [i["attn_conv_w"], i["attn_conv_b"][:, None], i["attn_dt_bias"][:, None], i["attn_D_param"][:, None], i["attn_A"]], axis=1)
    arrays = {
        "x": i["attn_hidden_states"].reshape(TOKENS, HID),
        "w_u": w_in[:CHAN].reshape(JT, P, KT, P).transpose(3, 0, 2, 1),
        "w_g": tiled(w_in[CHAN:].T, KT),
        "chan": tiled(per_channel, JT),
        "w_x": tiled(i["attn_Wx"].T, JT),
        "w_dt": i["attn_Wdt"].T,
        "rows": np.concatenate([i["attn_dt_ln_w"], i["attn_b_ln_w"], i["attn_c_ln_w"], i["ffn_gate_b"]])[None, :],
        "gate_w": tiled(i["ffn_gate_w"].T, KT),
        "exp_w": i["ffn_expert_w"].transpose(0, 2, 1).reshape(EXPERTS, KT, P, HID).transpose(0, 2, 1, 3),
        "exp_b": i["ffn_expert_b"],
        "w_out": tiled(i["attn_W_out"].T, JT),
        "consts": constants(),
    }
    arrays = {f"in_{k}": np.ascontiguousarray(v) for k, v in arrays.items()}
    nc = bacc.Bacc("TRN2", target_bir_lowering=False, num_devices=1)
    args = [nc.dram_tensor(k, v.shape, mybir.dt.from_np(v.dtype), kind="ExternalInput").ap() for k, v in arrays.items()]
    out = nc.dram_tensor("out", (TOKENS, HID), F32, kind="ExternalOutput").ap()
    ssm_moe_program(nc, *args, out)
    r = run_bass_kernel_spmd(nc, [arrays], core_ids=[0])
    return r.results[0]["out"].reshape(BATCHES, STEPS, HID)
```

```python
import concourse.bass as bass
from concourse import mybir
from contextlib import ExitStack

F32 = mybir.dt.float32
U32 = mybir.dt.uint32
ALU = mybir.AluOpType
ACT = mybir.ActivationFunctionType
AX = mybir.AxisListType

P = 128
BATCHES, STEPS, HID = 4, 256, 512
CHAN, STATES, TAPS, RANK = 1024, 16, 4, 32
SSM = RANK + 2 * STATES
EXPERTS = 8
TOKENS = BATCHES * STEPS
TT = TOKENS // P
TB = STEPS // P
KT = HID // P
JT = CHAN // P
UNITS = BATCHES * JT
NC = 4
CH = STATES // NC
CW = NC * STEPS
CHUNKS = UNITS * CH
GJ = 4
GW = TB * CHAN // GJ
ETILES = TT + EXPERTS - 1
SLOTS = ETILES * P
LN_EPS, RMS_EPS = 1e-5, 1e-6
SP_CAP = 40.0
PAIRS = UNITS // 2
BP = JT // 2

R_STATE, R_U, R_DELTA, R_YD = 6, 12, 4, 16

C_ID, C_TRI, C_ONE = 0, P, 2 * P
C_GRP = 3 * P
C_IOTA = C_GRP + SSM
C_IOTA8 = C_IOTA + EXPERTS
C_STEP = C_IOTA8 + EXPERTS
C_TILE = C_STEP + EXPERTS
C_MASK = C_TILE + ETILES
C_ALL = C_MASK + EXPERTS * TT
V_TAP, V_CB, V_DTB, V_D, V_A = 0, TAPS, TAPS + 1, TAPS + 2, TAPS + 3
V_ALL = V_A + STATES

SUM = 2
U_AT = ((), (11, 13, 14, 16), (0, 9, 15, 20), (5, 6, 13, 16))
G_AT = ((0, 1, 2), (3, 5, 9, 11), (5, 11, 16, 17), (1, 8, 9, 14))
X_AT = (0, 21, 22, 19)
SILU_AT = (3, 18, 21, 18)
E_AT = (17, 20, 23, 25, 28, 30, 32, 34, 37, 39, 41, 45, 52, 54, 56)
O_AT = ((60, 61, 62, 66), (74, 80, 87, 98), (106, 109, 114, 119))
GATHER_AT, SILU_ROWS_AT = (59, 69, 98), (62, 75, 102)
LAST_O_AT = (125, 127)
AFTER = dict(TA=1, UA=1, UC=1, GA=1, XA=1, EV=1, BA=1, OM=2, XS=1, XM=1, XR=2, XP=3, XN=3)
BEFORE = dict(D=6, DX=5, DE=3, DM=2)
XT_BEFORE, Y_AFTER, B_AFTER, LOGITS_AT = 2, 1, 2, 7
LAST = CHUNKS + SUM + 3


def timetable():
    at = {q: [] for q in range(-1, LAST + 1)}

    def put(q, *task):
        at[q].append(task)

    at[-1] = [("LN", 0), ("LN", 1), ("T", 0), ("T", 1), ("TA", 0), ("TA", 1),
              ("U", 0), ("UA", 0), ("UC", 0), ("U", 1), ("UA", 1), ("UC", 1), ("SU", 0),
              ("U", 2), ("UA", 2), ("UC", 2), ("SU", 1), ("U", 3), ("UA", 3), ("UC", 3), ("SU", 2), ("SU", 3),
              ("G", 0, 0), ("GA", 0, 0), ("LN", 2), ("X", 0), ("XS", 0), ("XM", 0), ("XR", 0), ("XP", 0), ("XN", 0),
              ("D", 0), ("DX", 0), ("DE", 0), ("DM", 0)]
    for i in range(UNITS):
        put(CH * (i + 1) + SUM - 1 + Y_AFTER, "Y", i)
    for p in range(PAIRS):
        base = 2 * CH * p
        if p:
            for stage, steps in BEFORE.items():
                put(base - steps, stage, p)
        put(base + 2 * CH + SUM + B_AFTER, "B", p)
        put(base + 2 * CH + SUM + B_AFTER + AFTER["BA"], "BA", p)
    for b in range(BATCHES):
        base = max(b - 1, 0) * CH * JT
        for n, r in enumerate(U_AT[b]):
            p = BP * b + n
            put(base + r, "U", p)
            put(base + r + AFTER["UA"], "UA", p)
            put(base + r + AFTER["UC"], "UC", p)
        for n, r in enumerate(G_AT[b]):
            g = GJ - len(G_AT[b]) + n
            put(base + r, "G", b, g)
            put(base + r + AFTER["GA"], "GA", b, g)
        if b:
            for n in range(BP):
                put(base + SILU_AT[b], "SU", BP * b + n)
            put(base + X_AT[b], "X", b)
            for stage in ("XS", "XM", "XR", "XP", "XN"):
                put(base + X_AT[b] + AFTER[stage], stage, b)
        put(base + SILU_AT[b], "SG", b)
    for t in range(2, TT):
        if t > 2:
            put(t - 3, "LN", t)
        put(t - 2, "T", t)
        put(t - 2 + AFTER["TA"], "TA", t)
    for n, stage in enumerate(("LOG", "CH", "RT", "RO")):
        put(LOGITS_AT + n, stage)
    for n in range(TT):
        put(LOGITS_AT + 4 + n // 2, "SC", n)
    for k, q in enumerate(E_AT):
        put(q - XT_BEFORE, "XT", k)
        put(q - XT_BEFORE + AFTER["XA"], "XA", k)
        put(q, "E", k)
        put(q + AFTER["EV"], "EV", k)
    for b, steps in enumerate(O_AT):
        put(GATHER_AT[b], "FG", b)
        if b == 2:
            put(GATHER_AT[b], "FG", 3)
        put(SILU_ROWS_AT[b], "SF", b)
        for n, q in enumerate(steps):
            put(q, "O", b, n // 2, n % 2)
            put(q + AFTER["OM"], "OM", b, n // 2, n % 2)
            if n % 2:
                put(q + AFTER["OM"], "OA", b, n // 2)
    for tt in range(TB):
        put(LAST_O_AT[tt], "OP", tt)
        put(LAST - 1, "OL", tt)
        put(LAST, "OF", tt)
    return at


TIMES = timetable()
PLAN = [(q, TIMES[q]) for q in range(-1, LAST + 1)]
ORDER = [t for _, ts in PLAN for t in ts]
PE_KINDS = ("T", "U", "X", "XM", "D", "G", "LOG", "RT", "XT", "E", "B", "O", "OP")
JOBS = [t for t in ORDER if t[0] in PE_KINDS and t != ("B", PAIRS - 1)]
JOB = {t: n for n, t in enumerate(JOBS)}


def ordinal(task):
    return [t for t in ORDER if t[0] == task[0]].index(task)


def ssm_moe_program(nc, x, w_u, w_g, chan, w_x, w_dt, norm_w, gate_b, gate_w, exp_w, exp_b, w_out, consts, out):
    xs = nc.dram_tensor("tokens_by_expert", (SLOTS, HID), F32, kind="Internal").ap()
    ys = nc.dram_tensor("expert_rows", (SLOTS, HID), F32, kind="Internal").ap()
    bc = nc.dram_tensor("bc_by_state", (BATCHES, 2 * STATES * STEPS), F32, kind="Internal").ap()

    ctx = ExitStack()
    with ctx:
        def sb(name, shape, dt=F32):
            return ctx.enter_context(nc.sbuf_tensor(name, shape, dt))

        def pb(name, shape):
            return ctx.enter_context(nc.psum_tensor(name, shape, F32))

        def sem(name):
            return ctx.enter_context(nc.semaphore(name))

        cst = sb("cst", [P, C_ALL])
        ident = cst[:, C_ID:C_ID + P]
        ch = sb("ch", [P, JT, V_ALL])
        rw = sb("rw", [P, EXPERTS])
        lnw = sb("lnw", [SSM, 1])
        wu = sb("wu", [P, JT, KT, P])
        wg = sb("wg", [P, KT, CHAN])
        wx = sb("wx", [P, JT, SSM])
        wdt = sb("wdt", [RANK, CHAN])
        gw = sb("gw", [P, KT, EXPERTS])
        shared = sb("shared", [P, TT * HID])
        xn = shared[:, :].rearrange("p (t h) -> p t h", t=TT)
        ew = shared[:, :].rearrange("p (s k h) -> p s k h", s=2, k=KT)
        wo = shared[:, :].rearrange("p (j h) -> p j h", j=JT)
        xnt = sb("xnt", [P, KT, TOKENS])
        ur = sb("ur", [P, R_U, STEPS])
        dl = sb("dl", [P, R_DELTA, STEPS])
        spx = sb("spx", [P, 2 * STEPS])
        ud = sb("ud", [P, 2, STEPS])
        st = sb("st", [P, R_STATE, CW])
        bb = sb("bb", [P, STATES * STEPS])
        cb = sb("cb", [P, STATES * STEPS])
        gt = sb("gt", [P, 2, TB, CHAN])
        ygt = sb("ygt", [P, 2, TB, P])
        yd = sb("yd", [P, R_YD, STEPS])
        xg = sb("xg", [P, 2, HID])
        xgt = sb("xgt", [P, KT, P])
        ebr = sb("ebr", [P, 2, HID])
        yr = sb("yr", [P, 2, HID])
        fg = sb("fg", [P, TB, HID])
        xr = sb("xr", [P, TB, HID])
        stats = sb("stats", [P, TT, 6])
        mv = sb("mv", [P, TT, 2])
        rstd = sb("rstd", [P, TT])
        half = sb("half", [P, 4])
        squares = sb("squares", [P, STEPS])
        sq = squares[0:SSM, :]
        nt = sb("nt", [SSM, STEPS])
        NE = EXPERTS * TT
        eq, cnt, tot, inc, lg, big = (spx[:, a:z] for a, z in (
            (0, NE), (NE, 3 * NE), (3 * NE, 4 * NE), (4 * NE, 5 * NE), (5 * NE, 6 * NE), (6 * NE, 6 * NE + ETILES * EXPERTS)))
        oneh = squares[:, 0:NE]
        s8 = squares[:, NE:2 * NE].rearrange("p (a e) -> p a e", e=EXPERTS)
        slot = sb("slot", [P, TT], U32)
        ek = sb("ek", [P, ETILES], U32)

        dA = [pb(f"dA{s}", [P, CW]) for s in range(2)]
        wp = pb("wp", [P, 2 * STEPS])
        yp = pb("yp", [P, 2 * STEPS])
        mp = [pb(f"mp{s}", [P, 2 * STEPS]) for s in range(2)]
        ysum = yp[:, 0:TB * P].rearrange("p (t c) -> p t c", t=TB)

        l_x = [sem(f"l_x{t}") for t in range(TT)]
        l_wu = [sem(f"l_wu{j}") for j in range(JT)]
        l_cst, l_ch, l_rw, l_lnw, l_wx, l_wdt, l_gw, l_wg, l_wo = (sem(n) for n in (
            "l_cst", "l_ch", "l_rw", "l_lnw", "l_wx", "l_wdt", "l_gw", "l_wg", "l_wo"))
        l_b = [sem(f"l_b{c}") for c in range(CH)]
        l_c = [sem(f"l_c{c}") for c in range(CH)]
        l_xg = [sem(f"l_xg{s}") for s in range(2)]
        l_e = [sem(f"l_e{s}") for s in range(2)]
        l_xr = [sem(f"l_xr{t}") for t in range(TB)]
        l_fg = [sem(f"l_fg{t}") for t in range(TT)]
        s_zero, s_bc, s_scat = sem("s_zero"), sem("s_bc"), sem("s_scat")
        s_ys = [sem(f"s_ys{s}") for s in range(2)]
        s_out = [sem(f"s_out{t}") for t in range(TB)]
        exp_done, wb_done, scan_done, cm_done, nsum_done = (sem(n) for n in (
            "exp_done", "wb_done", "scan_done", "cm_done", "nsum_done"))
        filled = {n: sem(f"filled_{n}") for n in PE_KINDS + ("OL",)}
        freed = {n: sem(f"freed_{n}") for n in PE_KINDS[:-1]}
        cleared, zeroed, const_half = sem("cleared"), sem("zeroed"), sem("const_half")
        var_done, rstd_done, xn_done = sem("var_done"), sem("rstd_done"), sem("xn_done")
        ua_done, tap_done = sem("ua_done"), sem("tap_done")
        silu_u, silu_g, silu_f, ud_done = sem("silu_u"), sem("silu_g"), sem("silu_f"), sem("ud_done")
        sq_done, ms_done = sem("sq_done"), sem("ms_done")
        rms_log, rms_done = sem("rms_log"), sem("rms_done")
        spx_done, spe_done, spl_done = sem("spx_done"), sem("spe_done"), sem("spl_done")
        delta_done, w_done = sem("delta_done"), sem("w_done")
        y_taken = sem("y_taken")
        oneh_done, routed = sem("oneh_done"), sem("routed")
        out_done, tail_mul, tail_done, chain = sem("out_done"), sem("tail_mul"), sem("tail_done"), sem("chain")

        block = ctx.enter_context(nc.Block())

        def state(q):
            return st[:, q % R_STATE, :].rearrange("p (n t) -> p n t", n=NC)

        def bank(task):
            return mp[JOB[task] % 2]

        def pair(ring, p, size):
            at = 2 * p % size
            return ring[:, at:at + 2, :].rearrange("p u t -> p (u t)")

        def rows_of(b, tt):
            return fg[:, tt, :] if b < 2 else gt[:, 0, b - 2, tt * HID:(tt + 1) * HID]

        @block.sync
        def _(sp):
            def x_tile(t):
                return x[t * P:(t + 1) * P, :]

            for t in range(2):
                sp.dma_start(xn[:, t, :], x_tile(t)).then_inc(l_x[t], 16)
            for j in range(JT):
                sp.dma_start(wu[:, j, :, :], w_u[:, j, :, :]).then_inc(l_wu[j], 16)
            for t in range(2, TB * 2):
                sp.dma_start(xn[:, t, :], x_tile(t)).then_inc(l_x[t], 16)
            sp.dma_start(wg[:, :, :], w_g).then_inc(l_wg, 16)
            for t in range(TB * 2, TT):
                sp.dma_start(xn[:, t, :], x_tile(t)).then_inc(l_x[t], 16)

            def store_bc(b):
                sp.wait_ge(freed["XM"], b + 1)
                sp.dma_start(bc[b].rearrange("(s t) -> s t", t=STEPS), nt[RANK:SSM, :]).then_inc(s_bc, 16)

            def load_bc(b, c, which):
                sp.wait_ge(s_bc, 16 * (b + 1))
                last = CH * JT * b - CH + c
                if which == 0:
                    if b:
                        sp.wait_ge(wb_done, last + 1)
                    src = bc[b, c * CW:(c + 1) * CW]
                    sp.dma_start(bb[:, c * CW:(c + 1) * CW], src.partition_broadcast(P)).then_inc(l_b[c], 16)
                else:
                    if b:
                        sp.wait_ge(cm_done, last + 1)
                    src = bc[b, (CH + c) * CW:(CH + c + 1) * CW]
                    sp.dma_start(cb[:, c * CW:(c + 1) * CW], src.partition_broadcast(P)).then_inc(l_c[c], 16)

            def load_expert_tokens(k):
                if k == 0:
                    sp.wait_ge(s_scat, 16 * TT)
                if k >= 2:
                    sp.wait_ge(filled["XT"], k - 1)
                sp.dma_start(xg[:, k % 2, :], xs[k * P:(k + 1) * P, :]).then_inc(l_xg[k % 2], 16)

            def load_expert_weights(k):
                s = k % 2
                if k == 0:
                    sp.wait_ge(s_scat, 16 * TT)
                    sp.wait_ge(freed["T"], TT)
                if k >= 2:
                    sp.wait_ge(filled["E"], k - 1)
                    sp.wait_ge(freed["E"], k - 1)
                e = sp.value_load(ek[0:1, k:k + 1], min_val=0, max_val=EXPERTS - 1)
                sp.dma_start(ew[:, s, :, :], exp_w[bass.ds(e, 1), :, :, :].rearrange("o p k h -> (o p) k h")).then_inc(l_e[s], 16)
                sp.dma_start(ebr[:, s, :], exp_b[bass.ds(e, 1), :].broadcast_to([P, HID])).then_inc(l_e[s], 16)

            def store_expert_tile(k):
                sp.wait_ge(freed["E"], k + 1)
                sp.dma_start(ys[k * P:(k + 1) * P, :], yr[:, k % 2, :]).then_inc(s_ys[k % 2], 16)

            def load_residual(b, tt):
                if b:
                    sp.wait_ge(s_out[tt], 16 * b)
                else:
                    sp.wait_ge(s_zero, 16)
                sp.dma_start(xr[:, tt, :], x_tile(TB * b + tt)).then_inc(l_xr[tt], 16)

            store_bc(0)
            for c in range(CH):
                load_bc(0, c, 0)
            for c in range(CH):
                load_bc(0, c, 1)
            for q, tasks in PLAN[1:]:
                b, r = divmod(q, CH * JT)
                if b + 1 < BATCHES and r >= 28:
                    load_bc(b + 1, r - 28, 0)
                if 1 <= b < BATCHES and r < CH:
                    load_bc(b, r, 1)
                for t in tasks:
                    if t[0] == "XN":
                        store_bc(t[1])
                    if t == ("SC", 0):
                        load_residual(0, 0)
                        load_residual(0, 1)
                    if t == ("SC", TT - 1):
                        sp.wait_ge(routed, 1)
                        for k in range(2):
                            load_expert_tokens(k)
                            load_expert_weights(k)
                    if t[0] == "XA" and t[1] + 2 < ETILES:
                        load_expert_tokens(t[1] + 2)
                    if t[0] == "EV":
                        store_expert_tile(t[1])
                        if t[1] + 2 < ETILES:
                            load_expert_weights(t[1] + 2)
                        if t[1] == ETILES - 1:
                            sp.wait_ge(filled["E"], ETILES)
                            sp.dma_start(wo, w_out).then_inc(l_wo, 16)
                    if t[0] in ("OA", "OF"):
                        ob, tt = t[1:] if t[0] == "OA" else (BATCHES - 1, t[1])
                        if t[0] == "OA":
                            sp.wait_ge(out_done, TB * ob + tt + 1)
                        else:
                            sp.wait_ge(tail_done, tt + 1)
                        row = (TB * ob + tt) * P
                        sp.dma_start(out[row:row + P, :], xr[:, tt, :]).then_inc(s_out[tt], 16)
                        if ob + 1 < BATCHES:
                            load_residual(ob + 1, tt)
            for tt in range(TB):
                sp.wait_ge(s_out[tt], 16 * BATCHES)

        @block.gpsimd
        def _(pool):
            pool.memset(half[:, :], -0.5).then_inc(const_half, 1)
            pool.wait_ge(const_half, 1)
            for q, tasks in PLAN:
                if q == 0:
                    pool.wait_ge(zeroed, 1)
                    pool.dma_start(xs.rearrange("(k p) h -> p k h", p=P),
                                   xr[:, 0:1, :].broadcast_to([P, ETILES, HID])).then_inc(s_zero, 16)
                if 0 <= q < CHUNKS:
                    i, c = divmod(q, CH)
                    pool.wait_ge(l_c[c], 16 * (i // JT + 1))
                    pool.wait_ge(scan_done, q + 1)
                    nc.gpsimd.tensor_tensor(st[:, q % R_STATE, :], st[:, q % R_STATE, :], cb[:, c * CW:(c + 1) * CW],
                                            ALU.mult).then_inc(cm_done, 1)
                for t in tasks:
                    if t[0] == "LN":
                        pool.wait_ge(var_done, t[1] + 1)
                        nc.gpsimd.tensor_tensor(rstd[:, t[1]:t[1] + 1], mv[:, t[1], 1:2], half[:, 0:1],
                                                ALU.pow).then_inc(rstd_done, 1)
                    if t[0] == "SC":
                        if t[1] == 0:
                            pool.wait_ge(routed, 1)
                            pool.wait_ge(s_zero, 16)
                            pool.wait_ge(xn_done, TT)
                        pool.indirect_dma_start(xs, bass.IndirectOffsetOnAxis(ap=slot[:, t[1]:t[1] + 1], axis=0),
                                                xn[:, t[1], :], None).then_inc(s_scat, 16)
                    if t[0] == "FG":
                        b = t[1]
                        if b == 0:
                            pool.wait_ge(s_ys[0], 16 * ((ETILES + 1) // 2))
                            pool.wait_ge(s_ys[1], 16 * (ETILES // 2))
                        if b == 1:
                            pool.wait_ge(out_done, TB * b)
                        if b == 2:
                            pool.wait_ge(y_taken, JT * (b + 1))
                        for tt in range(TB):
                            tile = TB * b + tt
                            pool.indirect_dma_start(rows_of(b, tt), None, ys,
                                                    bass.IndirectOffsetOnAxis(ap=slot[:, tile:tile + 1], axis=0)
                                                    ).then_inc(l_fg[tile], 16)
                    if t[0] == "OA":
                        _, b, tt = t
                        pool.wait_ge(freed["O"], 2 * (TB * b + tt + 1))
                        pool.wait_ge(l_xr[tt], 16 * (b + 1))
                        nc.gpsimd.tensor_tensor(xr[:, tt, :], xr[:, tt, :], rows_of(b, tt), ALU.add).then_inc(out_done, 1)

        @block.scalar
        def _(act):
            act.dma_start(cst[:, :], consts).then_inc(l_cst, 16)
            act.dma_start(ch[:, :, :], chan).then_inc(l_ch, 16)
            act.dma_start(wx[:, :, :], w_x).then_inc(l_wx, 16)
            act.dma_start(lnw[:, :], norm_w).then_inc(l_lnw, 16)
            act.dma_start(wdt[:, :], w_dt).then_inc(l_wdt, 16)
            act.dma_start(gw[:, :, :], gate_w).then_inc(l_gw, 16)
            act.dma_start(rw[:, :], gate_b.broadcast_to([P, EXPERTS])).then_inc(l_rw, 16)
            nc.scalar.preload_act_table_set("silu_and_others")
            act.wait_ge(l_ch, 16)

            def exps(q):
                i, c = divmod(q, CH)
                j = i % JT
                if q == 0:
                    act.wait_ge(cleared, 1)
                if c == 0:
                    act.wait_ge(delta_done, i // 2 + 1)
                if q >= 2:
                    act.wait_ge(scan_done, q - 1)
                for n in range(NC):
                    at = V_A + NC * c + n
                    last = nc.scalar.activation(dA[q % 2][:, n * STEPS + 1:(n + 1) * STEPS], dl[:, i % R_DELTA, 1:STEPS],
                                                ACT.Exp, scale=ch[:, j, at:at + 1])
                last.then_inc(exp_done, 1)

            def skip(i):
                act.wait_ge(silu_u, i // 2 + 1)
                if i >= 2:
                    act.wait_ge(nsum_done, CH * (i - 2) + 1)
                j = i % JT
                nc.scalar.activation(ud[:, i % 2, :], ur[:, i % R_U, :], ACT.Copy,
                                     scale=ch[:, j, V_D:V_D + 1]).then_inc(ud_done, 1)

            def table(name):
                nc.scalar.preload_act_table_set(name)

            silus = ("SU", "SG", "SF")
            for q, tasks in PLAN:
                if 0 <= q < CHUNKS:
                    if q == 0:
                        exps(0)
                        skip(0)
                    if q + 1 < CHUNKS:
                        exps(q + 1)
                        if (q + 1) % CH == 0:
                            skip((q + 1) // CH)
                for at, t in enumerate(tasks):
                    n = ordinal(t)
                    if q >= 0 and t[0] in silus and (not at or tasks[at - 1][0] not in silus):
                        table("silu_and_others")
                    job = {"TA": "T", "UA": "U", "XS": "X", "GA": "G", "XA": "XT", "BA": "B"}.get(t[0])
                    if job:
                        act.wait_ge(filled[job], n + 1)
                        m = dA[0][:, 0:2 * STEPS] if t == ("BA", PAIRS - 1) else bank((job,) + t[1:])
                    if t[0] == "TA":
                        nc.scalar.activation(xnt[:, :, t[1] * P:(t[1] + 1) * P],
                                             m[:, 0:KT * P].rearrange("p (k c) -> p k c", k=KT), ACT.Copy
                                             ).then_inc(freed["T"], 1)
                    if t[0] == "UA":
                        p = t[1]
                        if p >= R_U // 2:
                            before = p - R_U // 2
                            act.wait_ge(w_done, before + 1)
                            act.wait_ge(ud_done, 2 * before + 2)
                            act.wait_ge(filled["X"], before // BP + 1)
                        for h in range(2):
                            j = (2 * p + h) % JT
                            last = nc.scalar.activation(ur[:, (2 * p + h) % R_U, :], m[:, h * STEPS:(h + 1) * STEPS],
                                                        ACT.Identity, scale=ch[:, j, TAPS - 1:TAPS],
                                                        bias=ch[:, j, V_CB:V_CB + 1])
                        last.then_inc(ua_done, 1)
                    if t[0] == "XS":
                        b = t[1]
                        if b >= 1:
                            act.wait_ge(freed["XM"], b)
                            act.wait_ge(filled["D"], BP * b)
                            act.wait_ge(s_bc, 16 * b)
                        if b == 1:
                            act.wait_ge(routed, 1)
                        nc.scalar.activation(sq[:, :], m[0:SSM, 0:STEPS], ACT.Square).then_inc(sq_done, 1)
                        nc.scalar.activation(nt[:, :], m[0:SSM, 0:STEPS], ACT.Copy).then_inc(freed["X"], 1)
                    if t[0] == "XP":
                        act.wait_ge(ms_done, n + 1)
                        nc.scalar.activation(sq[:, :], sq[:, :], ACT.Ln).then_inc(rms_log, 1)
                        act.wait_ge(rms_log, n + 1)
                        nc.scalar.activation(sq[:, :], sq[:, :], ACT.Exp, scale=-0.5).then_inc(rms_done, 1)
                    if t[0] == "GA":
                        _, b, g = t
                        if b >= 2:
                            act.wait_ge(y_taken, JT * (b - 1))
                        tt, col = divmod(g * GW, CHAN)
                        nc.scalar.activation(gt[:, b % 2, tt, col:col + GW], m[:, 0:GW],
                                             ACT.Copy).then_inc(freed["G"], 1)
                    if t[0] == "XA":
                        if n:
                            act.wait_ge(filled["E"], n)
                        nc.scalar.activation(xgt[:, :, :], m[:, 0:KT * P].rearrange("p (k c) -> p k c", k=KT),
                                             ACT.Copy).then_inc(freed["XT"], 1)
                    if t[0] == "BA":
                        p = t[1]
                        if 2 * p >= R_YD:
                            act.wait_ge(filled["O"], 2 * TB * (p // BP - 1))
                        nc.scalar.activation(pair(yd, p, R_YD), m[:, 0:2 * STEPS], ACT.Copy).then_inc(freed["B"], 1)
                    if t[0] == "SU":
                        act.wait_ge(freed["U"], t[1] + 1)
                        u = pair(ur, t[1], R_U)
                        nc.scalar.activation(u, u, ACT.Silu).then_inc(silu_u, 1)
                    if t[0] == "SG":
                        b = t[1]
                        act.wait_ge(freed["G"], GJ * (b + 1))
                        g = gt[:, b % 2, :, :].rearrange("p t c -> p (t c)")
                        nc.scalar.activation(g, g, ACT.Silu).then_inc(silu_g, 1)
                    if t[0] == "SF":
                        b = t[1]
                        for tile in range(TB * b, TB * (b + 1) if b < 2 else TT):
                            act.wait_ge(l_fg[tile], 16)
                        f = (fg[:, :, :] if b < 2 else gt[:, 0, :, :]).rearrange("p t c -> p (t c)")
                        nc.scalar.activation(f, f, ACT.Silu).then_inc(silu_f, 1)
                    after = tasks[at + 1][0] if at + 1 < len(tasks) else None
                    if q >= 0 and t[0] in silus and after not in silus or t == ("SU", BP - 1):
                        table("natural_log_exp_and_others")
                    if t[0] == "DE":
                        p = t[1]
                        act.wait_ge(spx_done, p + 1)
                        nc.scalar.activation(spx[:, :], spx[:, :], ACT.Exp).then_inc(spe_done, 1)
                        act.wait_ge(spe_done, p + 1)
                        nc.scalar.activation(spx[:, :], spx[:, :], ACT.Ln, bias=1.0).then_inc(spl_done, 1)

        @block.vector
        def _(dve):
            links = [0]

            def link(ins):
                links[0] += 1
                ins.then_inc(chain, 1)
                dve.wait_ge(chain, links[0])

            nc.vector.memset(xr[:, 0, :], 0.0).then_inc(zeroed, 1)
            for s in range(2):
                last = nc.vector.memset(dA[s][:, 0:CW].rearrange("p (n t) -> p n t", n=NC)[:, :, 0:1], 0.0)
            last.then_inc(cleared, 1)

            def product(q):
                i, c = divmod(q, CH)
                dve.wait_ge(l_b[c], 16 * (i // JT + 1))
                dve.wait_ge(w_done, i // 2 + 1)
                if q >= R_STATE:
                    dve.wait_ge(nsum_done, q - R_STATE + 1)
                nc.vector.tensor_tensor(state(q), wp[:, (i % 2) * STEPS:(i % 2 + 1) * STEPS].unsqueeze(1).broadcast_to([P, NC, STEPS]),
                                        bb[:, c * CW:(c + 1) * CW].rearrange("p (n t) -> p n t", n=NC),
                                        ALU.mult).then_inc(wb_done, 1)

            def scan(q):
                dve.wait_ge(exp_done, q + 1)
                dve.wait_ge(wb_done, q + 1)
                nc.vector.tensor_tensor_scan(st[:, q % R_STATE, :], dA[q % 2][:, :], st[:, q % R_STATE, :], 0.0,
                                             ALU.mult, ALU.add).then_inc(scan_done, 1)

            def layernorm(t):
                dve.wait_ge(l_x[t], 16)
                link(nc.vector.bn_stats(stats[:, t, :], xn[:, t, :]))
                link(nc.vector.bn_aggr(mv[:, t, :], stats[:, t, :]))
                nc.vector.tensor_scalar(mv[:, t, 1:2], mv[:, t, 1:2], LN_EPS, None, ALU.add).then_inc(var_done, 1)
                dve.wait_ge(rstd_done, t + 1)
                nc.vector.tensor_scalar(xn[:, t, :], xn[:, t, :], mv[:, t, 0:1], rstd[:, t:t + 1],
                                        ALU.subtract, ALU.mult).then_inc(xn_done, 1)

            def conv(p, m):
                dve.wait_ge(ua_done, p + 1)
                for k in range(1, TAPS):
                    for h in range(2):
                        j = (2 * p + h) % JT
                        o = ur[:, (2 * p + h) % R_U, :]
                        if k > 1:
                            dve.wait_ge(tap_done, 2 * (TAPS - 2) * p + 2 * (k - 2) + h + 1)
                        ins = nc.vector.scalar_tensor_tensor(out=o[:, k:STEPS], in0=m[:, h * STEPS:(h + 1) * STEPS - k],
                                                             scalar=ch[:, j, TAPS - 1 - k:TAPS - k],
                                                             in1=o[:, k:STEPS], op0=ALU.mult, op1=ALU.add)
                        if k < TAPS - 1:
                            ins.then_inc(tap_done, 1)
                ins.then_inc(freed["U"], 1)

            def choose(m):
                def v(a):
                    return a[:, :].rearrange("p (t e) -> p t e", e=EXPERTS)

                def by_expert(a):
                    return a.unsqueeze(1).broadcast_to([P, TT, EXPERTS])

                def by_tile(a):
                    return a.unsqueeze(2).broadcast_to([P, TT, EXPERTS])
                nc.vector.tensor_tensor(v(lg), m[:, 0:NE].rearrange("p (t e) -> p t e", e=EXPERTS),
                                        by_expert(rw[:, :]), ALU.add).then_inc(freed["LOG"], 1)
                dve.wait_ge(freed["LOG"], 1)
                link(nc.vector.tensor_reduce(s8[:, 0, :], v(lg), AX.X, ALU.max))
                link(nc.vector.tensor_tensor(v(eq), v(lg), by_tile(s8[:, 0, :]), ALU.is_equal))
                link(nc.vector.scalar_tensor_tensor(out=v(eq), in0=v(eq), scalar=-float(EXPERTS),
                                                    in1=by_expert(cst[:, C_IOTA8:C_IOTA8 + EXPERTS]),
                                                    op0=ALU.mult, op1=ALU.add))
                link(nc.vector.tensor_reduce(s8[:, 1, :], v(eq), AX.X, ALU.min))
                nc.vector.tensor_tensor(v(oneh), by_expert(cst[:, C_IOTA:C_IOTA + EXPERTS]), by_tile(s8[:, 1, :]),
                                        ALU.is_equal).then_inc(oneh_done, 1)

            def route(m):
                nc.vector.tensor_copy(cnt[:, :], m[:, 0:2 * NE]).then_inc(freed["RT"], 1)
                dve.wait_ge(freed["RT"], 1)
                te, et = "p (t e) -> p t e", "p (e t) -> p e t"
                link(nc.vector.tensor_copy(tot[:, :].rearrange(et, e=EXPERTS),
                                           cnt[:, NE:2 * NE].rearrange("p (t e) -> p e t", e=EXPERTS)))
                link(nc.vector.tensor_tensor_scan(inc[:, :], cst[:, C_MASK:C_MASK + NE], tot[:, :], 0.0,
                                                  ALU.mult, ALU.add))
                link(nc.vector.tensor_tensor(tot[:, :], inc[:, :], tot[:, :], ALU.subtract))
                count = inc[:, :].rearrange(et, e=EXPERTS)[:, :, TT - 1:TT].broadcast_to([P, EXPERTS, TT])
                steps = cst[:, C_STEP:C_STEP + TT].unsqueeze(1).broadcast_to([P, EXPERTS, TT])
                link(nc.vector.tensor_tensor(eq[:, :].rearrange(et, e=EXPERTS), count, steps, ALU.is_gt))
                link(nc.vector.tensor_reduce(s8[:, 2, :], eq[:, :].rearrange(et, e=EXPERTS), AX.X, ALU.add))
                link(nc.vector.tensor_tensor_scan(s8[:, 3, :], cst[:, C_ONE:C_ONE + EXPERTS], s8[:, 2, :], 0.0,
                                                  ALU.mult, ALU.add))
                link(nc.vector.tensor_tensor(s8[:, 4, :], s8[:, 3, :], s8[:, 2, :], ALU.subtract))
                link(nc.vector.tensor_scalar(s8[:, 4, :], s8[:, 4, :], float(P), None, ALU.mult))
                rank = eq[:, :].rearrange(te, e=EXPERTS)
                link(nc.vector.tensor_tensor(rank, cnt[:, 0:NE].rearrange(te, e=EXPERTS),
                                             tot[:, :].rearrange("p (e t) -> p t e", e=EXPERTS), ALU.add))
                link(nc.vector.tensor_tensor(rank, rank, s8[:, 4, :].unsqueeze(1).broadcast_to([P, TT, EXPERTS]), ALU.add))
                link(nc.vector.tensor_tensor(eq[:, :], eq[:, :], oneh[:, :], ALU.mult))
                link(nc.vector.tensor_reduce(s8[:, 5, :], rank, AX.X, ALU.add))
                link(nc.vector.tensor_copy(slot[:, :], s8[:, 5, :]))
                cmp = big[:, :].rearrange("p (k e) -> p k e", e=EXPERTS)
                link(nc.vector.tensor_tensor(cmp, s8[:, 3, :].unsqueeze(1).broadcast_to([P, ETILES, EXPERTS]),
                                             cst[:, C_TILE:C_TILE + ETILES].unsqueeze(2).broadcast_to([P, ETILES, EXPERTS]),
                                             ALU.is_le))
                link(nc.vector.tensor_reduce(lg[:, 0:ETILES], cmp, AX.X, ALU.add))
                nc.vector.tensor_scalar(ek[:, :], lg[:, 0:ETILES], float(EXPERTS - 1), None, ALU.min).then_inc(routed, 1)

            def softplus_in(p, m):
                if p >= R_DELTA // 2:
                    dve.wait_ge(exp_done, 2 * CH * (p - 1))
                    dve.wait_ge(w_done, p - 1)
                if p:
                    dve.wait_ge(delta_done, p)
                if p == 2:
                    dve.wait_ge(routed, 1)
                for h in range(2):
                    j = (2 * p + h) % JT
                    last = nc.vector.tensor_scalar(dl[:, (2 * p + h) % R_DELTA, :], m[:, h * STEPS:(h + 1) * STEPS],
                                                   ch[:, j, V_DTB:V_DTB + 1], None, ALU.add)
                last.then_inc(freed["D"], 1)
                dve.wait_ge(freed["D"], p + 1)
                nc.vector.tensor_scalar(spx[:, :], pair(dl, p, R_DELTA), SP_CAP, None, ALU.min).then_inc(spx_done, 1)

            def softplus_out(p):
                d = pair(dl, p, R_DELTA)
                dve.wait_ge(spl_done, p + 1)
                nc.vector.tensor_tensor(d, d, spx[:, :], ALU.max).then_inc(delta_done, 1)
                dve.wait_ge(delta_done, p + 1)
                dve.wait_ge(silu_u, p + 1)
                if p:
                    dve.wait_ge(wb_done, 2 * CH * p)
                nc.vector.tensor_tensor(wp[:, :], d, pair(ur, p, R_U), ALU.mult).then_inc(w_done, 1)

            for q, tasks in PLAN:
                if 0 <= q < CHUNKS:
                    if q == 0:
                        product(0)
                    scan(q)
                    if q + 1 < CHUNKS:
                        product(q + 1)
                for t in tasks:
                    n = ordinal(t)
                    job = {"UC": "U", "XR": "XM", "CH": "LOG", "RO": "RT", "DX": "D", "EV": "E", "OM": "O"}.get(t[0])
                    if job:
                        dve.wait_ge(filled[job], n + 1)
                        m = bank((job,) + t[1:])
                    if t[0] == "LN":
                        layernorm(t[1])
                    if t[0] == "UC":
                        if n == 0:
                            dve.wait_ge(l_ch, 16)
                        conv(n, m)
                    if t[0] == "XR":
                        nc.vector.tensor_scalar(sq[:, :], m[0:SSM, 0:STEPS], RMS_EPS, None, ALU.add).then_inc(ms_done, 1)
                    if t[0] == "XN":
                        if n == 0:
                            dve.wait_ge(l_lnw, 16)
                            link(nc.vector.tensor_scalar(lnw[:, :], lnw[:, :], -0.5, None, ALU.mult))
                        dve.wait_ge(rms_done, n + 1)
                        dve.wait_ge(freed["X"], n + 1)
                        m = bank(("XM", t[1]))
                        r = m[0:SSM, STEPS:2 * STEPS]
                        link(nc.vector.scalar_tensor_tensor(out=r, in0=m[0:SSM, 0:STEPS], scalar=RMS_EPS, in1=sq,
                                                            op0=ALU.add, op1=ALU.mult))
                        link(nc.vector.tensor_tensor(r, r, sq, ALU.mult))
                        link(nc.vector.scalar_tensor_tensor(out=r, in0=r, scalar=-3.0, in1=sq, op0=ALU.add, op1=ALU.mult))
                        nc.vector.scalar_tensor_tensor(out=nt[:, :], in0=r, scalar=lnw[:, 0:1], in1=nt[:, :],
                                                       op0=ALU.mult, op1=ALU.mult).then_inc(freed["XM"], 1)
                    if t[0] == "CH":
                        dve.wait_ge(l_cst, 16)
                        dve.wait_ge(l_rw, 16)
                        choose(m)
                    if t[0] == "RO":
                        route(m)
                    if t[0] == "DX":
                        softplus_in(n, m)
                    if t[0] == "DM":
                        softplus_out(n)
                    if t[0] == "Y":
                        i = t[1]
                        b, j = divmod(i, JT)
                        dve.wait_ge(nsum_done, CH * (i + 1))
                        dve.wait_ge(silu_g, b + 1)
                        if i >= 2:
                            dve.wait_ge(filled["B"], i // 2)
                        nc.vector.tensor_tensor(ygt[:, i % 2, :, :], ysum, gt[:, b % 2, :, j * P:(j + 1) * P],
                                                ALU.mult).then_inc(y_taken, 1)
                    if t[0] == "EV":
                        if n >= 2:
                            dve.wait_ge(s_ys[n % 2], 16 * (n // 2))
                        nc.vector.tensor_tensor(yr[:, n % 2, :], m[:, 0:HID], ebr[:, n % 2, :],
                                                ALU.add).then_inc(freed["E"], 1)
                    if t[0] == "OM":
                        _, b, tt, h = t
                        cols = slice(h * STEPS, (h + 1) * STEPS)
                        dve.wait_ge(silu_f, min(b, 2) + 1)
                        f = rows_of(b, tt)[:, cols]
                        nc.vector.tensor_tensor(f, m[:, 0:STEPS], f, ALU.mult).then_inc(freed["O"], 1)
                    if t == ("OF", 0):
                        for tt in range(TB):
                            f = rows_of(BATCHES - 1, tt)
                            dve.wait_ge(filled["OL"], tt + 1)
                            nc.vector.tensor_tensor(f, bank(("OP", tt))[:, 0:HID], f, ALU.mult).then_inc(tail_mul, 1)
                        for tt in range(TB):
                            dve.wait_ge(tail_mul, tt + 1)
                            dve.wait_ge(l_xr[tt], 16 * BATCHES)
                            nc.vector.tensor_tensor(xr[:, tt, :], xr[:, tt, :], rows_of(BATCHES - 1, tt),
                                                    ALU.add).then_inc(tail_done, 1)

        @block.tensor
        def _(pe):
            def mm(o, l, r, start, stop):
                return nc.tensor.matmul(o, l, r, start=start, stop=stop, skip_group_check=True)

            def flip(o, src, start=True, stop=True):
                return nc.tensor.matmul(o, src, ident, is_transpose=True, start=start, stop=stop, skip_group_check=True)

            def sum_states(q):
                i, c = divmod(q, CH)
                if c == 0:
                    pe.wait_ge(ud_done, i + 1)
                    if i:
                        pe.wait_ge(y_taken, i)
                    for tt in range(TB):
                        flip(ysum[:, tt, :], ud[:, i % 2, tt * P:(tt + 1) * P], start=(tt == 0), stop=False)
                pe.wait_ge(cm_done, q + 1)
                for n in range(NC):
                    for tt in range(TB):
                        at = n * STEPS + tt * P
                        last = flip(ysum[:, tt, :], st[:, q % R_STATE, at:at + P], start=False,
                                    stop=(c == CH - 1 and n == NC - 1))
                last.then_inc(nsum_done, 1)

            pe.wait_ge(l_cst, 16)
            for q, tasks in PLAN:
                sum_last = (q - SUM) % CH == 0
                if not sum_last and 0 <= q - SUM < CHUNKS:
                    sum_states(q - SUM)
                for t in tasks:
                    if t[0] not in filled:
                        continue
                    n = ordinal(t)
                    if t in JOB:
                        if JOB[t] >= 2:
                            before = JOBS[JOB[t] - 2]
                            pe.wait_ge(freed[before[0]], ordinal(before) + 1)
                        m = bank(t)
                    if t[0] == "T":
                        pe.wait_ge(xn_done, n + 1)
                        for k in range(KT):
                            last = flip(m[:, k * P:(k + 1) * P], xn[:, t[1], k * P:(k + 1) * P])
                    if t[0] == "U":
                        p = t[1]
                        b = p // BP
                        pe.wait_ge(freed["T"], TB * (b + 1))
                        for h in range(2):
                            j = (2 * p + h) % JT
                            if b == 0:
                                pe.wait_ge(l_wu[j], 16)
                            for k in range(KT):
                                last = mm(m[:, h * STEPS:(h + 1) * STEPS], wu[:, j, k, :],
                                          xnt[:, k, b * STEPS:(b + 1) * STEPS], k == 0, k == KT - 1)
                    if t[0] == "X":
                        b = t[1]
                        if n == 0:
                            pe.wait_ge(l_wx, 16)
                        for j in range(JT):
                            if j % 2 == 0:
                                pe.wait_ge(silu_u, BP * b + j // 2 + 1)
                            last = mm(m[0:SSM, 0:STEPS], wx[:, j, :], ur[:, (JT * b + j) % R_U, :], j == 0, j == JT - 1)
                    if t[0] == "XM":
                        pe.wait_ge(sq_done, n + 1)
                        last = mm(m[0:SSM, 0:STEPS], cst[0:SSM, C_GRP:C_GRP + SSM], sq[:, :], True, True)
                    if t[0] == "D":
                        p = t[1]
                        b = p // BP
                        if n == 0:
                            pe.wait_ge(l_wdt, 16)
                        pe.wait_ge(freed["XM"], b + 1)
                        for h in range(2):
                            j = (2 * p + h) % JT
                            last = mm(m[:, h * STEPS:(h + 1) * STEPS], wdt[:, j * P:(j + 1) * P], nt[0:RANK, :], True, True)
                    if t[0] == "G":
                        _, b, g = t
                        if n == 0:
                            pe.wait_ge(l_wg, 16)
                        tt, col = divmod(g * GW, CHAN)
                        at = (TB * b + tt) * P
                        pe.wait_ge(freed["T"], TB * (b + 1))
                        for k in range(KT):
                            last = mm(m[:, 0:GW], xnt[:, k, at:at + P], wg[:, k, col:col + GW], k == 0, k == KT - 1)
                    if t[0] == "LOG":
                        pe.wait_ge(l_gw, 16)
                        pe.wait_ge(freed["T"], TT)
                        for tt in range(TT):
                            for k in range(KT):
                                last = mm(m[:, tt * EXPERTS:(tt + 1) * EXPERTS], xnt[:, k, tt * P:(tt + 1) * P], gw[:, k, :],
                                          k == 0, k == KT - 1)
                    if t[0] == "RT":
                        pe.wait_ge(oneh_done, 1)
                        mm(m[:, 0:NE], cst[:, C_TRI:C_TRI + P], oneh[:, :], True, True)
                        last = mm(m[:, NE:2 * NE], cst[:, C_ONE:C_ONE + P], oneh[:, :], True, True)
                    if t[0] == "XT":
                        pe.wait_ge(l_xg[n % 2], 16 * (n // 2 + 1))
                        for k in range(KT):
                            last = flip(m[:, k * P:(k + 1) * P], xg[:, n % 2, k * P:(k + 1) * P])
                    if t[0] == "E":
                        pe.wait_ge(freed["XT"], n + 1)
                        pe.wait_ge(l_e[n % 2], 32 * (n // 2 + 1))
                        for k in range(KT):
                            last = mm(m[:, 0:HID], xgt[:, k, :], ew[:, n % 2, k, :], k == 0, k == KT - 1)
                    if t[0] == "B":
                        p = t[1]
                        pe.wait_ge(y_taken, 2 * p + 2)
                        if p == PAIRS - 1:
                            m = dA[0]
                            pe.wait_ge(scan_done, CHUNKS - 1)
                        for h in range(2):
                            for tt in range(TB):
                                at = h * STEPS + tt * P
                                last = flip(m[:, at:at + P], ygt[:, h, tt, :])
                    if t[0] == "O":
                        _, b, tt, h = t
                        if n == 0:
                            pe.wait_ge(l_wo, 16)
                        pe.wait_ge(freed["B"], BP * (b + 1))
                        for j in range(JT):
                            last = mm(m[:, 0:STEPS], yd[:, (JT * b + j) % R_YD, tt * P:(tt + 1) * P],
                                      wo[:, j, h * STEPS:(h + 1) * STEPS], j == 0, j == JT - 1)
                    if t[0] in ("OP", "OL"):
                        tt, early = t[1], t[0] == "OP"
                        pe.wait_ge(freed["B"], PAIRS - 1 if early else PAIRS)
                        m = bank(("OP", tt))
                        for j in range(JT - 2) if early else (JT - 2, JT - 1):
                            last = mm(m[:, 0:HID], yd[:, (JT * (BATCHES - 1) + j) % R_YD, tt * P:(tt + 1) * P],
                                      wo[:, j, :], j == 0, j == JT - 1)
                    last.then_inc(filled[t[0]], 1)
                if sum_last and 0 <= q - SUM < CHUNKS:
                    sum_states(q - SUM)


def constants():
    import numpy as np
    c = np.zeros((P, C_ALL), np.float32)
    c[:, C_ID:C_ID + P] = np.eye(P)
    c[:, C_TRI:C_TRI + P] = np.triu(np.ones((P, P)), 1)
    c[:, C_ONE:C_ONE + P] = 1
    for a, z in ((0, RANK), (RANK, RANK + STATES), (RANK + STATES, SSM)):
        c[a:z, C_GRP + a:C_GRP + z] = 1 / (z - a)
    c[:, C_IOTA:C_IOTA + EXPERTS] = np.arange(EXPERTS)
    c[:, C_IOTA8:C_IOTA8 + EXPERTS] = np.arange(EXPERTS) + EXPERTS
    c[:, C_STEP:C_STEP + TT] = np.arange(TT) * P
    c[:, C_TILE:C_TILE + ETILES] = np.arange(ETILES)
    c[:, C_MASK:C_MASK + EXPERTS * TT] = np.arange(EXPERTS * TT) % TT != 0
    return c


def kernel(**inputs):
    import numpy as np
    import concourse.bacc as bacc
    from concourse.bass_utils import run_bass_kernel_spmd

    i = {k.removeprefix("L0_"): np.asarray(v) for k, v in inputs.items()}

    def tiled(a, tiles):
        return a.reshape(tiles, P, -1).transpose(1, 0, 2)

    w_in = i["attn_W_in"]
    per_channel = np.concatenate(
        [i["attn_conv_w"], i["attn_conv_b"][:, None], i["attn_dt_bias"][:, None], i["attn_D_param"][:, None], i["attn_A"]], axis=1)
    arrays = {
        "x": i["attn_hidden_states"].reshape(TOKENS, HID),
        "w_u": w_in[:CHAN].reshape(JT, P, KT, P).transpose(3, 0, 2, 1),
        "w_g": tiled(w_in[CHAN:].T, KT),
        "chan": tiled(per_channel, JT),
        "w_x": tiled(i["attn_Wx"].T, JT),
        "w_dt": i["attn_Wdt"].T,
        "norm_w": np.concatenate([i["attn_dt_ln_w"], i["attn_b_ln_w"], i["attn_c_ln_w"]])[:, None],
        "gate_b": i["ffn_gate_b"][None, :],
        "gate_w": tiled(i["ffn_gate_w"].T, KT),
        "exp_w": i["ffn_expert_w"].transpose(0, 2, 1).reshape(EXPERTS, KT, P, HID).transpose(0, 2, 1, 3),
        "exp_b": i["ffn_expert_b"],
        "w_out": tiled(i["attn_W_out"].T, JT),
        "consts": constants(),
    }
    arrays = {f"in_{k}": np.ascontiguousarray(v) for k, v in arrays.items()}
    nc = bacc.Bacc("TRN2", target_bir_lowering=False, num_devices=1)
    args = [nc.dram_tensor(k, v.shape, mybir.dt.from_np(v.dtype), kind="ExternalInput").ap() for k, v in arrays.items()]
    out = nc.dram_tensor("out", (TOKENS, HID), F32, kind="ExternalOutput").ap()
    ssm_moe_program(nc, *args, out)
    r = run_bass_kernel_spmd(nc, [arrays], core_ids=[0])
    return r.results[0]["out"].reshape(BATCHES, STEPS, HID)
```

```python
import concourse.bass as bass
from concourse import mybir
from contextlib import ExitStack

F32 = mybir.dt.float32
U32 = mybir.dt.uint32
ALU = mybir.AluOpType
ACT = mybir.ActivationFunctionType
AX = mybir.AxisListType

P = 128
BATCHES, STEPS, HID = 4, 256, 512
CHAN, STATES, TAPS, RANK = 1024, 16, 4, 32
SSM = RANK + 2 * STATES
EXPERTS = 8
TOKENS = BATCHES * STEPS
TT = TOKENS // P
TB = STEPS // P
KT = HID // P
JT = CHAN // P
UNITS = BATCHES * JT
NC = 4
CH = STATES // NC
CW = NC * STEPS
CHUNKS = UNITS * CH
GJ = 4
GW = TB * CHAN // GJ
ETILES = TT + EXPERTS - 1
SLOTS = ETILES * P
LN_EPS, RMS_EPS = 1e-5, 1e-6
PAIRS = UNITS // 2
BP = JT // 2

R_STATE, R_U, R_DELTA, R_YD = 6, 12, 4, 16

C_ID, C_TRI, C_ONE = 0, P, 2 * P
C_GRP = 3 * P
C_IOTA = C_GRP + SSM
C_IOTA8 = C_IOTA + EXPERTS
C_STEP = C_IOTA8 + EXPERTS
C_TILE = C_STEP + EXPERTS
C_MASK = C_TILE + ETILES
C_ALL = C_MASK + EXPERTS * TT
V_TAP, V_CB, V_DTB, V_D, V_A = 0, TAPS, TAPS + 1, TAPS + 2, TAPS + 3
V_ALL = V_A + STATES

SUM = 2
U_AT = ((), (2, 4, 9, 20), (0, 3, 6, 19), (3, 15, 17, 18))
G_AT = ((3, 4), (6, 8, 11, 19), (1, 4, 10, 18), (4, 6, 13, 17))
X_AT = (0, 23, 22, 22)
SILU_AT = (6, 23, 21, 21)
E_AT = (13, 15, 18, 21, 25, 27, 30, 31, 34, 39, 42, 45, 48, 52, 56)
O_AT = ((60, 65, 74, 75), (84, 87, 90, 101), (107, 113, 119, 121))
GATHER_AT, SILU_ROWS_AT = (58, 79, 100), (62, 85, 105)
LAST_O_AT = (116, 125)
AFTER = dict(TA=1, UA=2, UC=2, GA=1, XA=1, EV=1, BA=1, OM=2,
             XS=1, XM=1, XR=2, XP=2, XN=3)
BEFORE = dict(D=7, DX=6, DE=5, DP=5, DM=3)
XT_BEFORE, Y_AFTER, B_AFTER = 2, 1, 2
ROUTE_AT = (3, 3, 4, 4)
SCATTER_AT, SCATTER_EVERY = 5, 1
FIRST = ("XM", "XS", "UA", "FG", "OL", "E", "DP", "T", "XN", "G", "UC", "OM", "XR", "XP", "D", "XT", "X",
         "CH", "B", "LG", "U", "BL", "RT", "RO", "TA", "DE", "RP", "OF", "GA", "SC", "OA", "O", "DX", "SU",
         "OP", "LN", "XA", "Y", "BA", "BE", "DM", "EV", "OQ")
LAST = CHUNKS + SUM + Y_AFTER + 2


def timetable():
    at = {q: [] for q in range(-1, LAST + 1)}

    def put(q, *task):
        at[q].append(task)

    at[-1] = [("LN", 0), ("LN", 1), ("T", 0), ("T", 1), ("TA", 0), ("TA", 1), ("LN", 2), ("LN", 3), ("LN", 4),
              ("U", 0), ("UA", 0), ("UC", 0), ("U", 1), ("UA", 1), ("UC", 1), ("SU", 0), ("LN", 5),
              ("U", 2), ("UA", 2), ("UC", 2), ("SU", 1), ("U", 3), ("UA", 3), ("UC", 3), ("SU", 2), ("SU", 3),
              ("G", 0, 0), ("GA", 0, 0), ("LN", 6), ("LN", 7), ("X", 0), ("XS", 0), ("XM", 0), ("XR", 0),
              ("T", 2), ("XP", 0), ("TA", 2), ("XN", 0),
              ("D", 0), ("DX", 0), ("DE", 0), ("DP", 0), ("T", 3), ("LG", 0), ("LG", 1), ("DM", 0)]
    at[0] = [("TA", 3), ("G", 0, 1), ("T", 4), ("TA", 4), ("GA", 0, 1), ("T", 5), ("TA", 5),
             ("LG", 2), ("T", 6), ("TA", 6), ("T", 7), ("TA", 7), ("LG", 3), ("LG", 4)]
    at[1] = [("LG", 5)]
    at[2] = [("LG", 6), ("LG", 7)]
    for i in range(UNITS):
        put(CH * (i + 1) + SUM - 1 + Y_AFTER, "Y", i)
    for p in range(PAIRS):
        base = 2 * CH * p
        if p:
            for stage, steps in BEFORE.items():
                put(base - steps, stage, p)
        if p < PAIRS - 1:
            put(base + 2 * CH + SUM + B_AFTER, "B", p)
            put(base + 2 * CH + SUM + B_AFTER + AFTER["BA"], "BA", p)
    for b in range(BATCHES):
        base = max(b - 1, 0) * CH * JT
        for n, r in enumerate(U_AT[b]):
            p = BP * b + n
            put(base + r, "U", p)
            put(base + r + AFTER["UA"], "UA", p)
            put(base + r + AFTER["UC"], "UC", p)
        for n, r in enumerate(G_AT[b]):
            g = GJ - len(G_AT[b]) + n
            put(base + r, "G", b, g)
            put(base + r + AFTER["GA"], "GA", b, g)
        if b:
            for n in range(BP):
                put(base + SILU_AT[b], "SU", BP * b + n)
            put(base + X_AT[b], "X", b)
            for stage in ("XS", "XM", "XR", "XP", "XN"):
                put(base + X_AT[b] + AFTER[stage], stage, b)
        put(base + SILU_AT[b], "SG", b)
    for q, stage in zip(ROUTE_AT, ("CH", "RT", "RO", "RP")):
        put(q, stage)
    for n in range(TT):
        put(SCATTER_AT + n * SCATTER_EVERY // 2, "SC", n)
    for k, q in enumerate(E_AT):
        put(q - XT_BEFORE, "XT", k)
        put(q - XT_BEFORE + AFTER["XA"], "XA", k)
        put(q, "E", k)
        put(q + AFTER["EV"], "EV", k)
    for b, steps in enumerate(O_AT):
        put(GATHER_AT[b], "FG", b)
        if b == 2:
            put(GATHER_AT[b], "FG", 3)
        put(SILU_ROWS_AT[b], "SF", b)
        for n, q in enumerate(steps):
            put(q, "O", b, n // 2, n % 2)
            put(q + AFTER["OM"], "OM", b, n // 2, n % 2)
            if n % 2:
                put(q + AFTER["OM"], "OA", b, n // 2)
    end = CHUNKS + SUM + Y_AFTER
    for h, q in enumerate((end - CH, end)):
        put(q, "BL", h)
        put(q + 1, "BE", h)
    put(end - 2, "OQ")
    put(end + 1, "OL")
    put(end + 2, "OF")
    for tt in range(TB):
        put(LAST_O_AT[tt], "OP", tt)
    for q in range(1, LAST + 1):
        at[q].sort(key=lambda t: FIRST.index("SU" if t[0] in ("SG", "SF") else t[0]))
    return at


TIMES = timetable()
PLAN = [(q, TIMES[q]) for q in range(-1, LAST + 1)]
ORDER = [t for _, ts in PLAN for t in ts]
PE_KINDS = ("T", "U", "X", "XM", "D", "G", "RT", "XT", "E", "B", "O", "OP")
JOBS = [t for t in ORDER if t[0] in PE_KINDS]
BANK, BEFORE_IN_BANK, _had = {}, {}, [None, None]
for _t in JOBS:
    _b = 1 - BANK[("OP", 0)] if ("OP", 0) in BANK else len(BANK) % 2
    BANK[_t], BEFORE_IN_BANK[_t], _had[_b] = _b, _had[_b], _t


def ordinal(task):
    return [t for t in ORDER if t[0] == task[0]].index(task)


def ssm_moe_program(nc, x, w_u, w_g, chan, w_x, w_dt, norm_w, gate_b, gate_w, exp_w, exp_b, w_out, consts, out):
    xs = nc.dram_tensor("tokens_by_expert", (SLOTS, HID), F32, kind="Internal").ap()
    ys = nc.dram_tensor("expert_rows", (SLOTS, HID), F32, kind="Internal").ap()
    bc = nc.dram_tensor("bc_by_state", (BATCHES, 2 * STATES * STEPS), F32, kind="Internal").ap()

    ctx = ExitStack()
    with ctx:
        def sb(name, shape, dt=F32):
            return ctx.enter_context(nc.sbuf_tensor(name, shape, dt))

        def pb(name, shape):
            return ctx.enter_context(nc.psum_tensor(name, shape, F32))

        def sem(name):
            return ctx.enter_context(nc.semaphore(name))

        cst = sb("cst", [P, C_ALL])
        ident = cst[:, C_ID:C_ID + P]
        ch = sb("ch", [P, JT, V_ALL])
        rw = sb("rw", [P, EXPERTS])
        lnw = sb("lnw", [SSM, 1])
        wu = sb("wu", [P, JT, KT, P])
        wg = sb("wg", [P, KT, CHAN])
        wx = sb("wx", [P, JT, SSM])
        wdt = sb("wdt", [RANK, CHAN])
        gw = sb("gw", [P, KT, EXPERTS])
        shared = sb("shared", [P, TT * HID])
        xn = shared[:, :].rearrange("p (t h) -> p t h", t=TT)
        ew = shared[:, :].rearrange("p (s k h) -> p s k h", s=2, k=KT)
        wo = shared[:, :].rearrange("p (j h) -> p j h", j=JT)
        xnt = sb("xnt", [P, KT, TOKENS])
        ur = sb("ur", [P, R_U, STEPS])
        dl = sb("dl", [P, R_DELTA, STEPS])
        spx = sb("spx", [P, 2 * STEPS])
        ud = sb("ud", [P, 2, STEPS])
        st = sb("st", [P, R_STATE, CW])
        bb = sb("bb", [P, STATES * STEPS])
        cb = sb("cb", [P, STATES * STEPS])
        gt = sb("gt", [P, 2, TB, CHAN])
        ygt = sb("ygt", [P, 2, TB, P])
        yd = sb("yd", [P, R_YD, STEPS])
        xg = sb("xg", [P, 2, HID])
        xgt = sb("xgt", [P, KT, P])
        ebr = sb("ebr", [P, 2, HID])
        yr = sb("yr", [P, 2, HID])
        fg = sb("fg", [P, TB, HID])
        xr = sb("xr", [P, TB, HID])
        stats = sb("stats", [P, TT, 6])
        mv = sb("mv", [P, TT, 2])
        rstd = sb("rstd", [P, TT])
        half = sb("half", [P, 4])
        sq = sb("sq", [SSM, STEPS])[:, :]
        nt = sb("nt", [SSM, STEPS])
        NE = EXPERTS * TT
        at, scratch = 0, {}
        for name, size in (("eq", NE), ("cnt", 2 * NE), ("tot", NE), ("inc", NE), ("lg", NE), ("oneh", NE),
                           ("s8", 8 * EXPERTS), ("big", ETILES * EXPERTS)):
            scratch[name] = fg[:, :, :].rearrange("p t h -> p (t h)")[:, at:at + size]
            at += size
        eq, cnt, tot, inc, lg, oneh, big = (scratch[n] for n in ("eq", "cnt", "tot", "inc", "lg", "oneh", "big"))
        s8 = scratch["s8"].rearrange("p (a e) -> p a e", e=EXPERTS)
        slot = sb("slot", [P, TT], U32)
        ek = sb("ek", [P, ETILES], U32)

        dA = [pb(f"dA{s}", [P, CW]) for s in range(2)]
        wp = pb("wp", [P, 2 * STEPS])
        yp = pb("yp", [P, 2 * STEPS])
        mp = [pb(f"mp{s}", [P, 2 * STEPS]) for s in range(2)]
        logits = yp[:, TB * P:TB * P + TT * EXPERTS]
        ysum = yp[:, 0:TB * P].rearrange("p (t c) -> p t c", t=TB)

        l_x = [sem(f"l_x{t}") for t in range(TT)]
        l_wu = [sem(f"l_wu{j}") for j in range(JT)]
        l_cst, l_ch, l_rw, l_lnw, l_wx, l_wdt, l_gw, l_wg, l_wo = (sem(n) for n in (
            "l_cst", "l_ch", "l_rw", "l_lnw", "l_wx", "l_wdt", "l_gw", "l_wg", "l_wo"))
        l_b = [sem(f"l_b{c}") for c in range(CH)]
        l_c = [sem(f"l_c{c}") for c in range(CH)]
        l_xg = [sem(f"l_xg{s}") for s in range(2)]
        l_e = [sem(f"l_e{s}") for s in range(2)]
        l_xr = [sem(f"l_xr{t}") for t in range(TB)]
        l_fg = [sem(f"l_fg{t}") for t in range(TT)]
        s_zero, s_bc, s_scat = sem("s_zero"), sem("s_bc"), sem("s_scat")
        s_ys = [sem(f"s_ys{s}") for s in range(2)]
        s_out = [sem(f"s_out{t}") for t in range(TB)]
        exp_done, wb_done, scan_done, cm_done, nsum_done = (sem(n) for n in (
            "exp_done", "wb_done", "scan_done", "cm_done", "nsum_done"))
        filled = {n: sem(f"filled_{n}") for n in PE_KINDS + ("LG", "BL", "OQ", "OL")}
        freed = {n: sem(f"freed_{n}") for n in PE_KINDS[:-1] + ("LG", "BL")}
        cleared, zeroed, const_half = sem("cleared"), sem("zeroed"), sem("const_half")
        var_done, rstd_done, xn_done = sem("var_done"), sem("rstd_done"), sem("xn_done")
        ua_done, tap_done = sem("ua_done"), sem("tap_done")
        silu_u, silu_g, silu_f, ud_done = sem("silu_u"), sem("silu_g"), sem("silu_f"), sem("ud_done")
        sq_done, ms_done = sem("sq_done"), sem("ms_done")
        rms_log, rms_done = sem("rms_log"), sem("rms_done")
        spx_done, spe_done, spl_done = sem("spx_done"), sem("spe_done"), sem("spl_done")
        delta_done, w_done = sem("delta_done"), sem("w_done")
        y_taken = sem("y_taken")
        oneh_done, routed = sem("oneh_done"), sem("routed")
        out_done, tail_mul, tail_done, chain = sem("out_done"), sem("tail_mul"), sem("tail_done"), sem("chain")

        block = ctx.enter_context(nc.Block())

        def state(q):
            return st[:, q % R_STATE, :].rearrange("p (n t) -> p n t", n=NC)

        def bank(task):
            return mp[BANK[task]]

        def pair(ring, p, size):
            at = 2 * p % size
            return ring[:, at:at + 2, :].rearrange("p u t -> p (u t)")

        last_pair = wp[:, 0:STEPS], dA[0][:, 0:STEPS]

        def rows_of(b, tt):
            return fg[:, tt, :] if b < 2 else gt[:, 0, b - 2, tt * HID:(tt + 1) * HID]

        @block.sync
        def _(sp):
            def x_tile(t):
                return x[t * P:(t + 1) * P, :]

            for t in range(2):
                sp.dma_start(xn[:, t, :], x_tile(t)).then_inc(l_x[t], 16)
            for j in range(JT):
                sp.dma_start(wu[:, j, :, :], w_u[:, j, :, :]).then_inc(l_wu[j], 16)
                if j in (1, 3, 4):
                    t = {1: 2, 3: 3, 4: 4}[j]
                    sp.dma_start(xn[:, t, :], x_tile(t)).then_inc(l_x[t], 16)
            for t in range(5, TT):
                sp.dma_start(xn[:, t, :], x_tile(t)).then_inc(l_x[t], 16)
            sp.dma_start(wg[:, :, :], w_g).then_inc(l_wg, 16)

            def store_bc(b):
                sp.wait_ge(freed["XM"], b + 1)
                sp.dma_start(bc[b].rearrange("(s t) -> s t", t=STEPS), nt[RANK:SSM, :]).then_inc(s_bc, 16)

            def load_bc(b, c, which):
                sp.wait_ge(s_bc, 16 * (b + 1))
                last = CH * JT * b - CH + c
                if which == 0:
                    if b:
                        sp.wait_ge(wb_done, last + 1)
                    src = bc[b, c * CW:(c + 1) * CW]
                    sp.dma_start(bb[:, c * CW:(c + 1) * CW], src.partition_broadcast(P)).then_inc(l_b[c], 16)
                else:
                    if b:
                        sp.wait_ge(cm_done, last + 1)
                    src = bc[b, (CH + c) * CW:(CH + c + 1) * CW]
                    sp.dma_start(cb[:, c * CW:(c + 1) * CW], src.partition_broadcast(P)).then_inc(l_c[c], 16)

            def load_expert_tokens(k):
                if k == 0:
                    sp.wait_ge(s_scat, 16 * TT)
                if k >= 2:
                    sp.wait_ge(filled["XT"], k - 1)
                sp.dma_start(xg[:, k % 2, :], xs[k * P:(k + 1) * P, :]).then_inc(l_xg[k % 2], 16)

            def load_expert_weights(k):
                s = k % 2
                if k == 0:
                    sp.wait_ge(s_scat, 16 * TT)
                    sp.wait_ge(freed["T"], TT)
                if k >= 2:
                    sp.wait_ge(filled["E"], k - 1)
                    sp.wait_ge(freed["E"], k - 1)
                e = sp.value_load(ek[0:1, k:k + 1], min_val=0, max_val=EXPERTS - 1)
                sp.dma_start(ew[:, s, :, :], exp_w[bass.ds(e, 1), :, :, :].rearrange("o p k h -> (o p) k h")).then_inc(l_e[s], 16)
                sp.dma_start(ebr[:, s, :], exp_b[bass.ds(e, 1), :].broadcast_to([P, HID])).then_inc(l_e[s], 16)

            def store_expert_tile(k):
                sp.wait_ge(freed["E"], k + 1)
                sp.dma_start(ys[k * P:(k + 1) * P, :], yr[:, k % 2, :]).then_inc(s_ys[k % 2], 16)

            def load_residual(b, tt):
                if b:
                    sp.wait_ge(s_out[tt], 16 * b)
                else:
                    sp.wait_ge(s_zero, 16)
                sp.dma_start(xr[:, tt, :], x_tile(TB * b + tt)).then_inc(l_xr[tt], 16)

            store_bc(0)
            for c in range(CH):
                load_bc(0, c, 0)
            for c in range(CH):
                load_bc(0, c, 1)
            for q, tasks in PLAN[1:]:
                b, r = divmod(q, CH * JT)
                if b + 1 < BATCHES and r >= 28:
                    load_bc(b + 1, r - 28, 0)
                if 1 <= b < BATCHES and r < CH:
                    load_bc(b, r, 1)
                for t in tasks:
                    if t[0] == "XN":
                        store_bc(t[1])
                    if t == ("SC", 0):
                        load_residual(0, 0)
                        load_residual(0, 1)
                    if t == ("SC", TT - 1):
                        sp.wait_ge(routed, 1)
                        for k in range(2):
                            load_expert_tokens(k)
                            load_expert_weights(k)
                    if t[0] == "XA" and t[1] + 2 < ETILES:
                        load_expert_tokens(t[1] + 2)
                    if t[0] == "EV":
                        store_expert_tile(t[1])
                        if t[1] + 2 < ETILES:
                            load_expert_weights(t[1] + 2)
                        if t[1] == ETILES - 1:
                            sp.wait_ge(filled["E"], ETILES)
                            sp.dma_start(wo, w_out).then_inc(l_wo, 16)
                    if t[0] == "OA":
                        _, ob, tt = t
                        sp.wait_ge(out_done, TB * ob + tt + 1)
                        row = (TB * ob + tt) * P
                        sp.dma_start(out[row:row + P, :], xr[:, tt, :]).then_inc(s_out[tt], 16)
                    if t[0] == "O" and t[1] and t[2:] == (0, 0):
                        load_residual(t[1], 0)
                        load_residual(t[1], 1)
                    if t == ("OP", 1):
                        load_residual(BATCHES - 1, 0)
                        load_residual(BATCHES - 1, 1)
            for tt, done in ((1, tail_done), (0, out_done)):
                sp.wait_ge(done, 1 if tt else TB * (BATCHES - 1) + 1)
                row = (TB * (BATCHES - 1) + tt) * P
                sp.dma_start(out[row:row + P, :], xr[:, tt, :]).then_inc(s_out[tt], 16)
            for tt in range(TB):
                sp.wait_ge(s_out[tt], 16 * BATCHES)

        @block.gpsimd
        def _(pool):
            pool.memset(half[:, :], -0.5).then_inc(const_half, 1)
            pool.wait_ge(const_half, 1)
            for q, tasks in PLAN:
                if 0 <= q < CHUNKS:
                    i, c = divmod(q, CH)
                    pool.wait_ge(l_c[c], 16 * (i // JT + 1))
                    pool.wait_ge(scan_done, q + 1)
                    nc.gpsimd.tensor_tensor(st[:, q % R_STATE, :], st[:, q % R_STATE, :], cb[:, c * CW:(c + 1) * CW],
                                            ALU.mult).then_inc(cm_done, 1)
                for t in tasks:
                    if t[0] == "LN":
                        pool.wait_ge(var_done, t[1] + 1)
                        nc.gpsimd.tensor_tensor(rstd[:, t[1]:t[1] + 1], mv[:, t[1], 1:2], half[:, 0:1],
                                                ALU.pow).then_inc(rstd_done, 1)
                    if t == ("LN", 5):
                        pool.wait_ge(zeroed, 1)
                        pool.dma_start(xs.rearrange("(k p) h -> p k h", p=P),
                                       xr[:, 0:1, :].broadcast_to([P, ETILES, HID])).then_inc(s_zero, 16)
                    if t[0] == "DP":
                        p = t[1]
                        pool.wait_ge(spl_done, p + 1)
                        pool.wait_ge(freed["D"], p + 1)
                        d = pair(dl, p, R_DELTA)
                        nc.gpsimd.tensor_tensor(d, d, spx[:, :], ALU.add).then_inc(delta_done, 1)
                    if t[0] == "SC":
                        if t[1] == 0:
                            pool.wait_ge(routed, 1)
                            pool.wait_ge(s_zero, 16)
                            pool.wait_ge(xn_done, TT)
                        pool.indirect_dma_start(xs, bass.IndirectOffsetOnAxis(ap=slot[:, t[1]:t[1] + 1], axis=0),
                                                xn[:, t[1], :], None).then_inc(s_scat, 16)
                    if t[0] == "FG":
                        b = t[1]
                        if b == 0:
                            pool.wait_ge(s_ys[0], 16 * ((ETILES + 1) // 2))
                            pool.wait_ge(s_ys[1], 16 * (ETILES // 2))
                        if b == 1:
                            pool.wait_ge(out_done, TB * b)
                        if b == 2:
                            pool.wait_ge(y_taken, JT * (b + 1))
                        for tt in range(TB):
                            tile = TB * b + tt
                            pool.indirect_dma_start(rows_of(b, tt), None, ys,
                                                    bass.IndirectOffsetOnAxis(ap=slot[:, tile:tile + 1], axis=0)
                                                    ).then_inc(l_fg[tile], 16)
                    if t[0] == "OA":
                        _, b, tt = t
                        pool.wait_ge(freed["O"], 2 * (TB * b + tt + 1))
                        pool.wait_ge(l_xr[tt], 16 * (b + 1))
                        nc.gpsimd.tensor_tensor(xr[:, tt, :], xr[:, tt, :], rows_of(b, tt), ALU.add).then_inc(out_done, 1)
                    if t[0] == "OF":
                        pool.wait_ge(tail_mul, 1)
                        pool.wait_ge(l_xr[0], 16 * BATCHES)
                        nc.gpsimd.tensor_tensor(xr[:, 0, :], xr[:, 0, :], rows_of(BATCHES - 1, 0), ALU.add).then_inc(out_done, 1)

        @block.scalar
        def _(act):
            act.dma_start(cst[:, :], consts).then_inc(l_cst, 16)
            act.dma_start(ch[:, :, :], chan).then_inc(l_ch, 16)
            act.dma_start(wx[:, :, :], w_x).then_inc(l_wx, 16)
            act.dma_start(lnw[:, :], norm_w).then_inc(l_lnw, 16)
            act.dma_start(wdt[:, :], w_dt).then_inc(l_wdt, 16)
            act.dma_start(gw[:, :, :], gate_w).then_inc(l_gw, 16)
            act.dma_start(rw[:, :], gate_b.broadcast_to([P, EXPERTS])).then_inc(l_rw, 16)
            nc.scalar.preload_act_table_set("silu_and_others")
            act.wait_ge(l_ch, 16)

            def exps(q):
                i, c = divmod(q, CH)
                j = i % JT
                if q == 0:
                    act.wait_ge(cleared, 1)
                if c == 0:
                    act.wait_ge(delta_done, i // 2 + 1)
                if q >= 2:
                    act.wait_ge(scan_done, q - 1)
                for n in range(NC):
                    at = V_A + NC * c + n
                    last = nc.scalar.activation(dA[q % 2][:, n * STEPS + 1:(n + 1) * STEPS], dl[:, i % R_DELTA, 1:STEPS],
                                                ACT.Exp, scale=ch[:, j, at:at + 1])
                last.then_inc(exp_done, 1)

            def skip(i):
                act.wait_ge(silu_u, i // 2 + 1)
                if i >= 2:
                    act.wait_ge(nsum_done, CH * (i - 2) + 1)
                j = i % JT
                nc.scalar.activation(ud[:, i % 2, :], ur[:, i % R_U, :], ACT.Copy,
                                     scale=ch[:, j, V_D:V_D + 1]).then_inc(ud_done, 1)

            def table(name):
                nc.scalar.preload_act_table_set(name)

            silus = ("SU", "SG", "SF")
            for q, tasks in PLAN:
                if 0 <= q < CHUNKS:
                    if q == 0:
                        exps(0)
                        skip(0)
                    if q + 1 < CHUNKS:
                        exps(q + 1)
                        if (q + 1) % CH == 0:
                            skip((q + 1) // CH)
                for at, t in enumerate(tasks):
                    n = ordinal(t)
                    if q >= 0 and t[0] in silus and (not at or tasks[at - 1][0] not in silus):
                        table("silu_and_others")
                    job = {"TA": "T", "UA": "U", "XS": "X", "GA": "G", "XA": "XT", "BA": "B", "DX": "D"}.get(t[0])
                    if job:
                        act.wait_ge(filled[job], n + 1)
                        m = bank((job,) + t[1:])
                    if t[0] == "TA":
                        nc.scalar.activation(xnt[:, :, t[1] * P:(t[1] + 1) * P],
                                             m[:, 0:KT * P].rearrange("p (k c) -> p k c", k=KT), ACT.Copy
                                             ).then_inc(freed["T"], 1)
                    if t[0] == "UA":
                        p = t[1]
                        if p >= R_U // 2:
                            before = p - R_U // 2
                            act.wait_ge(w_done, before + 1)
                            act.wait_ge(ud_done, 2 * before + 2)
                            act.wait_ge(filled["X"], before // BP + 1)
                        for h in range(2):
                            j = (2 * p + h) % JT
                            last = nc.scalar.activation(ur[:, (2 * p + h) % R_U, :], m[:, h * STEPS:(h + 1) * STEPS],
                                                        ACT.Identity, scale=ch[:, j, TAPS - 1:TAPS],
                                                        bias=ch[:, j, V_CB:V_CB + 1])
                        last.then_inc(ua_done, 1)
                    if t[0] == "XS":
                        b = t[1]
                        if b >= 1:
                            act.wait_ge(freed["XM"], b)
                            act.wait_ge(filled["D"], BP * b)
                            act.wait_ge(s_bc, 16 * b)
                        nc.scalar.activation(sq[:, :], m[0:SSM, 0:STEPS], ACT.Square).then_inc(sq_done, 1)
                        nc.scalar.activation(nt[:, :], m[0:SSM, 0:STEPS], ACT.Copy).then_inc(freed["X"], 1)
                    if t[0] == "XP":
                        act.wait_ge(ms_done, n + 1)
                        nc.scalar.activation(sq[:, :], sq[:, :], ACT.Ln).then_inc(rms_log, 1)
                        act.wait_ge(rms_log, n + 1)
                        nc.scalar.activation(sq[:, :], sq[:, :], ACT.Exp, scale=-0.5).then_inc(rms_done, 1)
                    if t[0] == "GA":
                        _, b, g = t
                        if b >= 2:
                            act.wait_ge(y_taken, JT * (b - 1))
                        tt, col = divmod(g * GW, CHAN)
                        nc.scalar.activation(gt[:, b % 2, tt, col:col + GW], m[:, 0:GW],
                                             ACT.Copy).then_inc(freed["G"], 1)
                    if t[0] == "XA":
                        if n:
                            act.wait_ge(filled["E"], n)
                        nc.scalar.activation(xgt[:, :, :], m[:, 0:KT * P].rearrange("p (k c) -> p k c", k=KT),
                                             ACT.Copy).then_inc(freed["XT"], 1)
                    if t[0] == "BA":
                        p = t[1]
                        if 2 * p >= R_YD:
                            act.wait_ge(filled["O"], 2 * TB * (p // BP - 1))
                        nc.scalar.activation(pair(yd, p, R_YD), m[:, 0:2 * STEPS], ACT.Copy).then_inc(freed["B"], 1)
                    if t[0] == "BE":
                        act.wait_ge(filled["BL"], t[1] + 1)
                        nc.scalar.activation(yd[:, (UNITS - 2 + t[1]) % R_YD, :], last_pair[t[1]], ACT.Copy
                                             ).then_inc(freed["BL"], 1)
                    if t[0] == "SU":
                        act.wait_ge(freed["U"], t[1] + 1)
                        u = pair(ur, t[1], R_U)
                        nc.scalar.activation(u, u, ACT.Silu).then_inc(silu_u, 1)
                    if t[0] == "SG":
                        b = t[1]
                        act.wait_ge(freed["G"], GJ * (b + 1))
                        g = gt[:, b % 2, :, :].rearrange("p t c -> p (t c)")
                        nc.scalar.activation(g, g, ACT.Silu).then_inc(silu_g, 1)
                    if t[0] == "SF":
                        b = t[1]
                        for tile in range(TB * b, TB * (b + 1) if b < 2 else TT):
                            act.wait_ge(l_fg[tile], 16)
                        f = (fg[:, :, :] if b < 2 else gt[:, 0, :, :]).rearrange("p t c -> p (t c)")
                        nc.scalar.activation(f, f, ACT.Silu).then_inc(silu_f, 1)
                    after = tasks[at + 1][0] if at + 1 < len(tasks) else None
                    if q >= 0 and t[0] in silus and after not in silus or t == ("SU", BP - 1):
                        table("natural_log_exp_and_others")
                    if t[0] == "DX":
                        p = t[1]
                        if p >= R_DELTA // 2:
                            act.wait_ge(exp_done, 2 * CH * (p - 1))
                            act.wait_ge(w_done, p - 1)
                        if p:
                            act.wait_ge(delta_done, p)
                        for func in (ACT.Abs, ACT.Relu):
                            for h in range(2):
                                j = (2 * p + h) % JT
                                o = spx[:, h * STEPS:(h + 1) * STEPS] if func == ACT.Abs else dl[:, (2 * p + h) % R_DELTA, :]
                                last = nc.scalar.activation(o, m[:, h * STEPS:(h + 1) * STEPS], func,
                                                            bias=ch[:, j, V_DTB:V_DTB + 1])
                            if func == ACT.Abs:
                                last.then_inc(spx_done, 1)
                        last.then_inc(freed["D"], 1)
                    if t[0] == "DE":
                        p = t[1]
                        act.wait_ge(spx_done, p + 1)
                        nc.scalar.activation(spx[:, :], spx[:, :], ACT.Exp, scale=-1.0).then_inc(spe_done, 1)
                        act.wait_ge(spe_done, p + 1)
                        nc.scalar.activation(spx[:, :], spx[:, :], ACT.Ln, bias=1.0).then_inc(spl_done, 1)

        @block.vector
        def _(dve):
            links = [0]

            def link(ins):
                links[0] += 1
                ins.then_inc(chain, 1)
                dve.wait_ge(chain, links[0])

            nc.vector.memset(xr[:, 0, :], 0.0).then_inc(zeroed, 1)
            for s in range(2):
                last = nc.vector.memset(dA[s][:, 0:CW].rearrange("p (n t) -> p n t", n=NC)[:, :, 0:1], 0.0)
            last.then_inc(cleared, 1)

            def product(q):
                i, c = divmod(q, CH)
                dve.wait_ge(l_b[c], 16 * (i // JT + 1))
                dve.wait_ge(w_done, i // 2 + 1)
                if q >= R_STATE:
                    dve.wait_ge(nsum_done, q - R_STATE + 1)
                nc.vector.tensor_tensor(state(q), wp[:, (i % 2) * STEPS:(i % 2 + 1) * STEPS].unsqueeze(1).broadcast_to([P, NC, STEPS]),
                                        bb[:, c * CW:(c + 1) * CW].rearrange("p (n t) -> p n t", n=NC),
                                        ALU.mult).then_inc(wb_done, 1)

            def scan(q):
                dve.wait_ge(exp_done, q + 1)
                dve.wait_ge(wb_done, q + 1)
                nc.vector.tensor_tensor_scan(st[:, q % R_STATE, :], dA[q % 2][:, :], st[:, q % R_STATE, :], 0.0,
                                             ALU.mult, ALU.add).then_inc(scan_done, 1)

            def layernorm(t):
                dve.wait_ge(l_x[t], 16)
                link(nc.vector.bn_stats(stats[:, t, :], xn[:, t, :]))
                link(nc.vector.bn_aggr(mv[:, t, :], stats[:, t, :]))
                nc.vector.tensor_scalar(mv[:, t, 1:2], mv[:, t, 1:2], LN_EPS, None, ALU.add).then_inc(var_done, 1)
                dve.wait_ge(rstd_done, t + 1)
                nc.vector.tensor_scalar(xn[:, t, :], xn[:, t, :], mv[:, t, 0:1], rstd[:, t:t + 1],
                                        ALU.subtract, ALU.mult).then_inc(xn_done, 1)

            def conv(p, m):
                dve.wait_ge(ua_done, p + 1)
                for k in range(1, TAPS):
                    for h in range(2):
                        j = (2 * p + h) % JT
                        o = ur[:, (2 * p + h) % R_U, :]
                        if k > 1:
                            dve.wait_ge(tap_done, 2 * (TAPS - 2) * p + 2 * (k - 2) + h + 1)
                        ins = nc.vector.scalar_tensor_tensor(out=o[:, k:STEPS], in0=m[:, h * STEPS:(h + 1) * STEPS - k],
                                                             scalar=ch[:, j, TAPS - 1 - k:TAPS - k],
                                                             in1=o[:, k:STEPS], op0=ALU.mult, op1=ALU.add)
                        if k < TAPS - 1:
                            ins.then_inc(tap_done, 1)
                ins.then_inc(freed["U"], 1)

            def choose(m):
                def v(a):
                    return a[:, :].rearrange("p (t e) -> p t e", e=EXPERTS)

                def by_expert(a):
                    return a.unsqueeze(1).broadcast_to([P, TT, EXPERTS])

                def by_tile(a):
                    return a.unsqueeze(2).broadcast_to([P, TT, EXPERTS])
                nc.vector.tensor_tensor(v(lg), m[:, 0:NE].rearrange("p (t e) -> p t e", e=EXPERTS),
                                        by_expert(rw[:, :]), ALU.add).then_inc(freed["LG"], 1)
                dve.wait_ge(freed["LG"], 1)
                link(nc.vector.tensor_reduce(s8[:, 0, :], v(lg), AX.X, ALU.max))
                link(nc.vector.tensor_tensor(v(eq), v(lg), by_tile(s8[:, 0, :]), ALU.is_equal))
                link(nc.vector.scalar_tensor_tensor(out=v(eq), in0=v(eq), scalar=-float(EXPERTS),
                                                    in1=by_expert(cst[:, C_IOTA8:C_IOTA8 + EXPERTS]),
                                                    op0=ALU.mult, op1=ALU.add))
                link(nc.vector.tensor_reduce(s8[:, 1, :], v(eq), AX.X, ALU.min))
                nc.vector.tensor_tensor(v(oneh), by_expert(cst[:, C_IOTA:C_IOTA + EXPERTS]), by_tile(s8[:, 1, :]),
                                        ALU.is_equal).then_inc(oneh_done, 1)

            def route(m):
                nc.vector.tensor_copy(cnt[:, :], m[:, 0:2 * NE]).then_inc(freed["RT"], 1)
                dve.wait_ge(freed["RT"], 1)
                et = "p (e t) -> p e t"
                link(nc.vector.tensor_copy(tot[:, :].rearrange(et, e=EXPERTS),
                                           cnt[:, NE:2 * NE].rearrange("p (t e) -> p e t", e=EXPERTS)))
                link(nc.vector.tensor_tensor_scan(inc[:, :], cst[:, C_MASK:C_MASK + NE], tot[:, :], 0.0,
                                                  ALU.mult, ALU.add))
                link(nc.vector.tensor_tensor(tot[:, :], inc[:, :], tot[:, :], ALU.subtract))
                count = inc[:, :].rearrange(et, e=EXPERTS)[:, :, TT - 1:TT].broadcast_to([P, EXPERTS, TT])
                steps = cst[:, C_STEP:C_STEP + TT].unsqueeze(1).broadcast_to([P, EXPERTS, TT])
                link(nc.vector.tensor_tensor(eq[:, :].rearrange(et, e=EXPERTS), count, steps, ALU.is_gt))
                link(nc.vector.tensor_reduce(s8[:, 2, :], eq[:, :].rearrange(et, e=EXPERTS), AX.X, ALU.add))
                link(nc.vector.tensor_tensor_scan(s8[:, 3, :], cst[:, C_ONE:C_ONE + EXPERTS], s8[:, 2, :], 0.0,
                                                  ALU.mult, ALU.add))
                link(nc.vector.tensor_tensor(s8[:, 4, :], s8[:, 3, :], s8[:, 2, :], ALU.subtract))
                link(nc.vector.tensor_scalar(s8[:, 4, :], s8[:, 4, :], float(P), None, ALU.mult))

            def place():
                te = "p (t e) -> p t e"
                rank = eq[:, :].rearrange(te, e=EXPERTS)
                link(nc.vector.tensor_tensor(rank, cnt[:, 0:NE].rearrange(te, e=EXPERTS),
                                             tot[:, :].rearrange("p (e t) -> p t e", e=EXPERTS), ALU.add))
                link(nc.vector.tensor_tensor(rank, rank, s8[:, 4, :].unsqueeze(1).broadcast_to([P, TT, EXPERTS]), ALU.add))
                link(nc.vector.tensor_tensor(eq[:, :], eq[:, :], oneh[:, :], ALU.mult))
                link(nc.vector.tensor_reduce(s8[:, 5, :], rank, AX.X, ALU.add))
                link(nc.vector.tensor_copy(slot[:, :], s8[:, 5, :]))
                cmp = big[:, :].rearrange("p (k e) -> p k e", e=EXPERTS)
                link(nc.vector.tensor_tensor(cmp, s8[:, 3, :].unsqueeze(1).broadcast_to([P, ETILES, EXPERTS]),
                                             cst[:, C_TILE:C_TILE + ETILES].unsqueeze(2).broadcast_to([P, ETILES, EXPERTS]),
                                             ALU.is_le))
                link(nc.vector.tensor_reduce(lg[:, 0:ETILES], cmp, AX.X, ALU.add))
                nc.vector.tensor_scalar(ek[:, :], lg[:, 0:ETILES], float(EXPERTS - 1), None, ALU.min).then_inc(routed, 1)

            def delta_u(p):
                d = pair(dl, p, R_DELTA)
                dve.wait_ge(delta_done, p + 1)
                dve.wait_ge(silu_u, p + 1)
                if p:
                    dve.wait_ge(wb_done, 2 * CH * p)
                nc.vector.tensor_tensor(wp[:, :], d, pair(ur, p, R_U), ALU.mult).then_inc(w_done, 1)

            for q, tasks in PLAN:
                if 0 <= q < CHUNKS:
                    if q == 0:
                        product(0)
                    scan(q)
                    if q == 0:
                        product(1)
                    if q + 2 < CHUNKS:
                        product(q + 2)
                for t in tasks:
                    n = ordinal(t)
                    job = {"UC": "U", "XR": "XM", "RO": "RT", "EV": "E", "OM": "O"}.get(t[0])
                    if job:
                        dve.wait_ge(filled[job], n + 1)
                        m = bank((job,) + t[1:])
                    if t[0] == "LN":
                        layernorm(t[1])
                    if t[0] == "UC":
                        if n == 0:
                            dve.wait_ge(l_ch, 16)
                        conv(n, m)
                    if t[0] == "XR":
                        nc.vector.tensor_scalar(sq[:, :], m[0:SSM, 0:STEPS], RMS_EPS, None, ALU.add).then_inc(ms_done, 1)
                    if t[0] == "XN":
                        if n == 0:
                            dve.wait_ge(l_lnw, 16)
                            link(nc.vector.tensor_scalar(lnw[:, :], lnw[:, :], -0.5, None, ALU.mult))
                        dve.wait_ge(rms_done, n + 1)
                        dve.wait_ge(freed["X"], n + 1)
                        m = bank(("XM", t[1]))
                        r = m[0:SSM, STEPS:2 * STEPS]
                        link(nc.vector.scalar_tensor_tensor(out=r, in0=m[0:SSM, 0:STEPS], scalar=RMS_EPS, in1=sq,
                                                            op0=ALU.add, op1=ALU.mult))
                        link(nc.vector.tensor_tensor(r, r, sq, ALU.mult))
                        link(nc.vector.scalar_tensor_tensor(out=r, in0=r, scalar=-3.0, in1=sq, op0=ALU.add, op1=ALU.mult))
                        nc.vector.scalar_tensor_tensor(out=nt[:, :], in0=r, scalar=lnw[:, 0:1], in1=nt[:, :],
                                                       op0=ALU.mult, op1=ALU.mult).then_inc(freed["XM"], 1)
                    if t[0] == "CH":
                        dve.wait_ge(l_cst, 16)
                        dve.wait_ge(l_rw, 16)
                        dve.wait_ge(filled["LG"], TT)
                        choose(logits)
                    if t[0] == "RO":
                        route(m)
                    if t[0] == "RP":
                        place()
                    if t[0] == "DM":
                        delta_u(n)
                    if t[0] == "Y":
                        i = t[1]
                        b, j = divmod(i, JT)
                        dve.wait_ge(nsum_done, CH * (i + 1))
                        dve.wait_ge(silu_g, b + 1)
                        if i >= 2:
                            dve.wait_ge(filled["B"], i // 2)
                        nc.vector.tensor_tensor(ygt[:, i % 2, :, :], ysum, gt[:, b % 2, :, j * P:(j + 1) * P],
                                                ALU.mult).then_inc(y_taken, 1)
                    if t[0] == "EV":
                        if n >= 2:
                            dve.wait_ge(s_ys[n % 2], 16 * (n // 2))
                        nc.vector.tensor_tensor(yr[:, n % 2, :], m[:, 0:HID], ebr[:, n % 2, :],
                                                ALU.add).then_inc(freed["E"], 1)
                    if t[0] == "OM":
                        _, b, tt, h = t
                        cols = slice(h * STEPS, (h + 1) * STEPS)
                        dve.wait_ge(silu_f, min(b, 2) + 1)
                        f = rows_of(b, tt)[:, cols]
                        nc.vector.tensor_tensor(f, m[:, 0:STEPS], f, ALU.mult).then_inc(freed["O"], 1)
                    if t[0] == "OF":
                        dve.wait_ge(filled["OL"], 1)
                        dve.wait_ge(silu_f, 3)
                        for tt in range(TB):
                            f = rows_of(BATCHES - 1, tt)
                            nc.vector.tensor_tensor(f, bank(("OP", tt))[:, 0:HID], f, ALU.mult).then_inc(tail_mul, 1)
                        dve.wait_ge(tail_mul, TB)
                        dve.wait_ge(l_xr[1], 16 * BATCHES)
                        nc.vector.tensor_tensor(xr[:, 1, :], xr[:, 1, :], f, ALU.add).then_inc(tail_done, 1)

        @block.tensor
        def _(pe):
            def mm(o, l, r, start, stop):
                return nc.tensor.matmul(o, l, r, start=start, stop=stop, skip_group_check=True)

            def flip(o, src, start=True, stop=True):
                return nc.tensor.matmul(o, src, ident, is_transpose=True, start=start, stop=stop, skip_group_check=True)

            def sum_states(q):
                i, c = divmod(q, CH)
                if c == 0:
                    pe.wait_ge(ud_done, i + 1)
                    if i:
                        pe.wait_ge(y_taken, i)
                    else:
                        pe.wait_ge(freed["LG"], 1)
                    for tt in range(TB):
                        flip(ysum[:, tt, :], ud[:, i % 2, tt * P:(tt + 1) * P], start=(tt == 0), stop=False)
                pe.wait_ge(cm_done, q + 1)
                for n in range(NC):
                    for tt in range(TB):
                        at = n * STEPS + tt * P
                        last = flip(ysum[:, tt, :], st[:, q % R_STATE, at:at + P], start=False,
                                    stop=(c == CH - 1 and n == NC - 1))
                last.then_inc(nsum_done, 1)

            pe.wait_ge(l_cst, 16)
            for q, tasks in PLAN:
                sum_last = (q - SUM) % CH == 0
                if not sum_last and 0 <= q - SUM < CHUNKS:
                    sum_states(q - SUM)
                for t in tasks:
                    if t[0] not in filled:
                        continue
                    n = ordinal(t)
                    if t in BANK:
                        before = BEFORE_IN_BANK[t]
                        if before:
                            pe.wait_ge(freed[before[0]], ordinal(before) + 1)
                        m = bank(t)
                    if t[0] == "T":
                        pe.wait_ge(xn_done, n + 1)
                        for k in range(KT):
                            last = flip(m[:, k * P:(k + 1) * P], xn[:, t[1], k * P:(k + 1) * P])
                    if t[0] == "U":
                        p = t[1]
                        b = p // BP
                        pe.wait_ge(freed["T"], TB * (b + 1))
                        for h in range(2):
                            j = (2 * p + h) % JT
                            if b == 0:
                                pe.wait_ge(l_wu[j], 16)
                            for k in range(KT):
                                last = mm(m[:, h * STEPS:(h + 1) * STEPS], wu[:, j, k, :],
                                          xnt[:, k, b * STEPS:(b + 1) * STEPS], k == 0, k == KT - 1)
                    if t[0] == "X":
                        b = t[1]
                        if n == 0:
                            pe.wait_ge(l_wx, 16)
                        for j in range(JT):
                            if j % 2 == 0:
                                pe.wait_ge(silu_u, BP * b + j // 2 + 1)
                            last = mm(m[0:SSM, 0:STEPS], wx[:, j, :], ur[:, (JT * b + j) % R_U, :], j == 0, j == JT - 1)
                    if t[0] == "XM":
                        pe.wait_ge(sq_done, n + 1)
                        last = mm(m[0:SSM, 0:STEPS], cst[0:SSM, C_GRP:C_GRP + SSM], sq[:, :], True, True)
                    if t[0] == "D":
                        p = t[1]
                        b = p // BP
                        if n == 0:
                            pe.wait_ge(l_wdt, 16)
                        pe.wait_ge(freed["XM"], b + 1)
                        for h in range(2):
                            j = (2 * p + h) % JT
                            last = mm(m[:, h * STEPS:(h + 1) * STEPS], wdt[:, j * P:(j + 1) * P], nt[0:RANK, :], True, True)
                    if t[0] == "G":
                        _, b, g = t
                        if n == 0:
                            pe.wait_ge(l_wg, 16)
                        tt, col = divmod(g * GW, CHAN)
                        at = (TB * b + tt) * P
                        pe.wait_ge(freed["T"], TB * (b + 1))
                        for k in range(KT):
                            last = mm(m[:, 0:GW], xnt[:, k, at:at + P], wg[:, k, col:col + GW], k == 0, k == KT - 1)
                    if t[0] == "LG":
                        tt = t[1]
                        if n == 0:
                            pe.wait_ge(l_gw, 16)
                        pe.wait_ge(freed["T"], tt + 1)
                        for k in range(KT):
                            last = mm(logits[:, tt * EXPERTS:(tt + 1) * EXPERTS], xnt[:, k, tt * P:(tt + 1) * P], gw[:, k, :],
                                      k == 0, k == KT - 1)
                    if t[0] == "RT":
                        pe.wait_ge(oneh_done, 1)
                        mm(m[:, 0:NE], cst[:, C_TRI:C_TRI + P], oneh[:, :], True, True)
                        last = mm(m[:, NE:2 * NE], cst[:, C_ONE:C_ONE + P], oneh[:, :], True, True)
                    if t[0] == "XT":
                        pe.wait_ge(l_xg[n % 2], 16 * (n // 2 + 1))
                        for k in range(KT):
                            last = flip(m[:, k * P:(k + 1) * P], xg[:, n % 2, k * P:(k + 1) * P])
                    if t[0] == "E":
                        pe.wait_ge(freed["XT"], n + 1)
                        pe.wait_ge(l_e[n % 2], 32 * (n // 2 + 1))
                        for k in range(KT):
                            last = mm(m[:, 0:HID], xgt[:, k, :], ew[:, n % 2, k, :], k == 0, k == KT - 1)
                    if t[0] == "B":
                        p = t[1]
                        pe.wait_ge(y_taken, 2 * p + 2)
                        for h in range(2):
                            for tt in range(TB):
                                at = h * STEPS + tt * P
                                last = flip(m[:, at:at + P], ygt[:, h, tt, :])
                    if t[0] == "O":
                        _, b, tt, h = t
                        if n == 0:
                            pe.wait_ge(l_wo, 16)
                        pe.wait_ge(freed["B"], BP * (b + 1))
                        for j in range(JT):
                            last = mm(m[:, 0:STEPS], yd[:, (JT * b + j) % R_YD, tt * P:(tt + 1) * P],
                                      wo[:, j, h * STEPS:(h + 1) * STEPS], j == 0, j == JT - 1)
                    if t[0] == "BL":
                        h = t[1]
                        pe.wait_ge(y_taken, UNITS - 1 + h)
                        if h == 0:
                            pe.wait_ge(wb_done, CHUNKS)
                        else:
                            pe.wait_ge(scan_done, CHUNKS - 1)
                        for tt in range(TB):
                            last = flip(last_pair[h][:, tt * P:(tt + 1) * P], ygt[:, h, tt, :])
                    if t[0] in ("OP", "OQ", "OL"):
                        if t[0] == "OP":
                            pe.wait_ge(freed["B"], PAIRS - 2 + t[1])
                            parts = ((t[1], range(0, JT - 4 + 2 * t[1])),)
                        elif t[0] == "OQ":
                            pe.wait_ge(freed["BL"], 1)
                            parts = (0, range(JT - 4, JT - 1)), (1, range(JT - 2, JT - 1))
                        else:
                            pe.wait_ge(freed["BL"], 2)
                            parts = (0, (JT - 1,)), (1, (JT - 1,))
                        for tt, tiles in parts:
                            for j in tiles:
                                last = mm(bank(("OP", tt))[:, 0:HID],
                                          yd[:, (JT * (BATCHES - 1) + j) % R_YD, tt * P:(tt + 1) * P],
                                          wo[:, j, :], j == 0, j == JT - 1)
                    last.then_inc(filled[t[0]], 1)
                if sum_last and 0 <= q - SUM < CHUNKS:
                    sum_states(q - SUM)


def constants():
    import numpy as np
    c = np.zeros((P, C_ALL), np.float32)
    c[:, C_ID:C_ID + P] = np.eye(P)
    c[:, C_TRI:C_TRI + P] = np.triu(np.ones((P, P)), 1)
    c[:, C_ONE:C_ONE + P] = 1
    for a, z in ((0, RANK), (RANK, RANK + STATES), (RANK + STATES, SSM)):
        c[a:z, C_GRP + a:C_GRP + z] = 1 / (z - a)
    c[:, C_IOTA:C_IOTA + EXPERTS] = np.arange(EXPERTS)
    c[:, C_IOTA8:C_IOTA8 + EXPERTS] = np.arange(EXPERTS) + EXPERTS
    c[:, C_STEP:C_STEP + TT] = np.arange(TT) * P
    c[:, C_TILE:C_TILE + ETILES] = np.arange(ETILES)
    c[:, C_MASK:C_MASK + EXPERTS * TT] = np.arange(EXPERTS * TT) % TT != 0
    return c


def kernel(**inputs):
    import numpy as np
    import concourse.bacc as bacc
    from concourse.bass_utils import run_bass_kernel_spmd

    i = {k.removeprefix("L0_"): np.asarray(v) for k, v in inputs.items()}

    def tiled(a, tiles):
        return a.reshape(tiles, P, -1).transpose(1, 0, 2)

    w_in = i["attn_W_in"]
    per_channel = np.concatenate(
        [i["attn_conv_w"], i["attn_conv_b"][:, None], i["attn_dt_bias"][:, None], i["attn_D_param"][:, None], i["attn_A"]], axis=1)
    arrays = {
        "x": i["attn_hidden_states"].reshape(TOKENS, HID),
        "w_u": w_in[:CHAN].reshape(JT, P, KT, P).transpose(3, 0, 2, 1),
        "w_g": tiled(w_in[CHAN:].T, KT),
        "chan": tiled(per_channel, JT),
        "w_x": tiled(i["attn_Wx"].T, JT),
        "w_dt": i["attn_Wdt"].T,
        "norm_w": np.concatenate([i["attn_dt_ln_w"], i["attn_b_ln_w"], i["attn_c_ln_w"]])[:, None],
        "gate_b": i["ffn_gate_b"][None, :],
        "gate_w": tiled(i["ffn_gate_w"].T, KT),
        "exp_w": i["ffn_expert_w"].transpose(0, 2, 1).reshape(EXPERTS, KT, P, HID).transpose(0, 2, 1, 3),
        "exp_b": i["ffn_expert_b"],
        "w_out": tiled(i["attn_W_out"].T, JT),
        "consts": constants(),
    }
    arrays = {f"in_{k}": np.ascontiguousarray(v) for k, v in arrays.items()}
    nc = bacc.Bacc("TRN2", target_bir_lowering=False, num_devices=1)
    args = [nc.dram_tensor(k, v.shape, mybir.dt.from_np(v.dtype), kind="ExternalInput").ap() for k, v in arrays.items()]
    out = nc.dram_tensor("out", (TOKENS, HID), F32, kind="ExternalOutput").ap()
    ssm_moe_program(nc, *args, out)
    r = run_bass_kernel_spmd(nc, [arrays], core_ids=[0])
    return r.results[0]["out"].reshape(BATCHES, STEPS, HID)
```
